# Optimizing a Trainium2 kernel written in Bass

```python
import numpy as np
import jax
import jax.numpy as jnp

def _softmax(x, axis=-1):
    return jax.nn.softmax(x, axis=axis)
def _gelu(x):
    return jax.nn.gelu(x, approximate=True)
def _silu(x):
    return jax.nn.silu(x)
def _sigmoid(x):
    return jax.nn.sigmoid(x)
def _layernorm(x, axis=-1, eps=1e-5):
    m = jnp.mean(x, axis=axis, keepdims=True)
    v = jnp.var(x, axis=axis, keepdims=True)
    return (x - m) / jnp.sqrt(v + eps)
def _scatter_add(tgt, idx, src, axis=0):
    return tgt.at[idx].add(src)
def _segment_sum(src, seg, n):
    return jax.ops.segment_sum(src, seg, n)

kernel_name = 'mk_adj_resnorm_d2_adj_512_f27567'

def setup_inputs(seed: int = 0):
    np.random.seed(seed)
    _w = jnp.asarray
    def _rec_inputs():
        import jax
        import jax.numpy as jnp
        _gk = jax.random.key(seed)
        x = -0.0003929 + 0.9999 * jax.random.normal(jax.random.fold_in(_gk, 1), (128, 128, 512), jnp.float32)
        _w = (1.0 + jnp.arange(128, dtype=jnp.float32)) ** -0.5
        _w = _w / _w.mean()
        _pij = jnp.clip(0.0625 * _w[:, None] * _w[None, :], 0.0, 1.0)
        _a = jax.random.uniform(jax.random.fold_in(_gk, 2), (128, 128, 128)) < _pij
        _a = jnp.logical_or(_a, jnp.eye(128, dtype=bool))
        _af = _a.astype(jnp.float32)
        _af = _af * jax.random.uniform(jax.random.fold_in(_gk, 3), (128, 128, 128), jnp.float32, 0.05, 1)
        adj = _af
        return x, adj
    x, adj = _rec_inputs()
    def _L0_gnn_setup():
        import jax, jax.numpy as jnp
        import numpy as np
        EPS = 1e-06
        key = jax.random.key(seed)
        k1, k2, k3 = jax.random.split(key, 3)
        B, N, F, O = (8, 4096, 512, 512)
        x = jax.random.normal(k1, (B, N, F), dtype=jnp.float32)
        adj = jax.random.uniform(k2, (B, N, N), dtype=jnp.float32)
        W = jax.random.normal(k3, (O, 2 * F), dtype=jnp.float32) * (1.0 / np.sqrt(2 * F))
        return {'x': x, 'adj': adj, 'W': W}
    _L0_gnn_all = _L0_gnn_setup()
    _L0_gnn_in = {k: v for k, v in _L0_gnn_all.items() if k in ('W', )}
    del _L0_gnn_all

    def _L1_gnn_setup():
        import jax, jax.numpy as jnp
        import numpy as np
        EPS_LN = 1e-05

        def hypergraph_conv(x, adj, W, b):
            N, C, _ = adj.shape
            H = (adj != 0).astype(x.dtype)
            w = adj.reshape(N, -1)[:, :C]
            xw = jnp.einsum('ncd,hd->nch', x, W)
            Dn = jnp.einsum('nce,ne->nc', H, w)
            Dn = jnp.where(Dn > 0, 1.0 / Dn, 0.0)
            Be = H.sum(axis=1)
            Be = jnp.where(Be > 0, 1.0 / Be, 0.0)
            m = Be[:, :, None] * jnp.einsum('nce,nch->neh', H, xw)
            out = Dn[:, :, None] * jnp.einsum('nce,neh->nch', H, m)
            return out + b

        def layer_norm(x, g, b):
            mu = jnp.mean(x, axis=-1, keepdims=True)
            var = jnp.var(x, axis=-1, keepdims=True)
            return (x - mu) * jax.lax.rsqrt(var + EPS_LN) * g + b
        key = jax.random.key(seed)
        ks = jax.random.split(key, 4)
        N, C, Din, Dh, Dout = (16, 1024, 512, 1024, 512)
        x = jax.random.normal(ks[0], (N, C, Din), dtype=jnp.float32)
        adj = jax.random.uniform(ks[1], (N, C, C), dtype=jnp.float32, minval=0.1, maxval=1.0)
        W1 = jax.random.normal(ks[2], (Dh, Din), dtype=jnp.float32) * (1.0 / np.sqrt(Din))
        b1 = jnp.zeros((Dh,), dtype=jnp.float32)
        gamma = jnp.ones((Dh,), dtype=jnp.float32)
        beta = jnp.zeros((Dh,), dtype=jnp.float32)
        W2 = jax.random.normal(ks[3], (Dout, Dh), dtype=jnp.float32) * (1.0 / np.sqrt(Dh))
        b2 = jnp.zeros((Dout,), dtype=jnp.float32)
        return {'x': x, 'adj': adj, 'W1': W1, 'b1': b1, 'gamma': gamma, 'beta': beta, 'W2': W2, 'b2': b2}
    _L1_gnn_all = _L1_gnn_setup()
    _L1_gnn_in = {k: v for k, v in _L1_gnn_all.items() if k in ('W1', 'b1', 'gamma', 'beta', 'W2', 'b2', )}
    del _L1_gnn_all

    return {
        "x": x,
        "adj": adj,
        "L0_gnn_W": _L0_gnn_in["W"],
        "L1_gnn_W1": _L1_gnn_in["W1"],
        "L1_gnn_b1": _L1_gnn_in["b1"],
        "L1_gnn_gamma": _L1_gnn_in["gamma"],
        "L1_gnn_beta": _L1_gnn_in["beta"],
        "L1_gnn_W2": _L1_gnn_in["W2"],
        "L1_gnn_b2": _L1_gnn_in["b2"],
    }

def reference(x, adj, L0_gnn_W, L1_gnn_W1, L1_gnn_b1, L1_gnn_gamma, L1_gnn_beta, L1_gnn_W2, L1_gnn_b2):
    import jax
    import jax.numpy as jnp
    def _L0_gnn_ref(x, adj, W):
        import jax, jax.numpy as jnp
        import numpy as np
        EPS = 1e-06
        deg = jnp.sum(adj, axis=-1, keepdims=True)
        agg = jnp.einsum('bij,bjf->bif', adj, x) / jnp.maximum(deg, EPS)
        cat = jnp.concatenate([x, agg], axis=2)
        out = jnp.einsum('bnf,of->bno', cat, W)
        return jax.nn.relu(out)

    def _L1_gnn_ref(x, adj, W1, b1, gamma, beta, W2, b2):
        import jax, jax.numpy as jnp
        import numpy as np
        EPS_LN = 1e-05

        def hypergraph_conv(x, adj, W, b):
            N, C, _ = adj.shape
            H = (adj != 0).astype(x.dtype)
            w = adj.reshape(N, -1)[:, :C]
            xw = jnp.einsum('ncd,hd->nch', x, W)
            Dn = jnp.einsum('nce,ne->nc', H, w)
            Dn = jnp.where(Dn > 0, 1.0 / Dn, 0.0)
            Be = H.sum(axis=1)
            Be = jnp.where(Be > 0, 1.0 / Be, 0.0)
            m = Be[:, :, None] * jnp.einsum('nce,nch->neh', H, xw)
            out = Dn[:, :, None] * jnp.einsum('nce,neh->nch', H, m)
            return out + b

        def layer_norm(x, g, b):
            mu = jnp.mean(x, axis=-1, keepdims=True)
            var = jnp.var(x, axis=-1, keepdims=True)
            return (x - mu) * jax.lax.rsqrt(var + EPS_LN) * g + b
        h = jax.nn.relu(hypergraph_conv(x, adj, W1, b1))
        h = layer_norm(h, gamma, beta)
        y = hypergraph_conv(h, adj, W2, b2)
        return y + x

    x = _layernorm(x + _L0_gnn_ref(x, adj, L0_gnn_W), axis=-1)
    x = _layernorm(x + _L1_gnn_ref(x, adj, L1_gnn_W1, L1_gnn_b1, L1_gnn_gamma, L1_gnn_beta, L1_gnn_W2, L1_gnn_b2), axis=-1)
    return x


_drawn_inputs = setup_inputs


def setup_inputs(seed=0):
    import zlib

    import numpy as np

    out = dict(_drawn_inputs(seed))
    spreads = {'L1_gnn_b1': (0.0, 0.1),
     'L1_gnn_gamma': (1.0, 0.2),
     'L1_gnn_beta': (0.0, 0.1),
     'L1_gnn_b2': (0.0, 0.1)}
    factors = {}
    for name, (base, spread) in spreads.items():
        noise = np.random.default_rng([zlib.crc32(name.encode()), seed]).standard_normal(out[name].shape)
        drawn = base * np.exp(spread * noise) if base else spread * noise
        out[name] = jnp.asarray(drawn.astype(out[name].dtype))
    for name, factor in factors.items():
        out[name] = (out[name] * factor).astype(out[name].dtype)
    return out
```

```python
from contextlib import ExitStack

import concourse.bass as bass
from concourse import mybir

P = 128
BANK = 512

ALU = mybir.AluOpType
ACT = mybir.ActivationFunctionType
F32 = mybir.dt.float32
F32R = mybir.dt.float32r
AX_X = mybir.AxisListType.X

DEG_EPS = 1e-6
LN_EPS = 1e-5
TINY = 1.1754944e-38


def later(g, n):
    return not isinstance(g, int) or g >= n


def half(g, p):
    return (g - p) * 8 + 16


def two_layer_graph_kernel(nc, x, adj, W0, W1, b1, gamma, beta, W2, b2, out):
    GRAPHS, NODES, D = x.shape
    DH = W1.shape[0]
    KD = D // P
    KH = DH // P
    K0 = 2 * KD
    HALVES = DH // BANK
    assert NODES == P and D == BANK and GRAPHS % 2 == 0 and GRAPHS >= 6

    with ExitStack() as ctx:
        def sb(name, shape, dt=F32):
            return ctx.enter_context(nc.sbuf_tensor(name, shape, dt))

        def sem(name):
            return ctx.enter_context(nc.semaphore(name))

        w0_hi = sb("w0_hi", [P, K0, D], F32R)
        w0_lo = sb("w0_lo", [P, K0, D], F32R)
        w1_hi = sb("w1_hi", [P, KD, DH], F32R)
        w1_lo = sb("w1_lo", [P, KD, DH], F32R)
        w2_hi = sb("w2_hi", [P, KH, D], F32R)
        w2_lo = sb("w2_lo", [P, KH, D], F32R)
        stage_a = sb("stage_a", [P, 4 * 1024])
        stage_b = sb("stage_b", [P, 4 * 1024])
        vec_rows = sb("vec_rows", [2 * KH, P])
        vec_cols = sb("vec_cols", [P, 2 * KH])
        beta_wide = sb("beta_wide", [P, KH, P])
        ident = sb("ident", [P, P])
        ones = sb("ones", [P, P])
        eps_col = sb("eps_col", [P, 1])
        b1_all = sb("b1_all", [P, DH])
        b2_all = sb("b2_all", [P, D])
        v_all = sb("v_all", [P, D])

        x_in = sb("x_in", [P, 2, D])
        adj_in = sb("adj_in", [P, 2, P])
        adj_norm = sb("adj_norm", [P, P])
        deg = sb("deg", [P, 3])
        adjT_norm = sb("adjT_norm", [P, P])
        incT = sb("incT", [P, P])
        count = sb("count", [P, 3])
        incT_be = sb("incT_be", [P, P + 2])
        G = sb("G", [P, 2, P])
        dsum = sb("dsum", [P, 2])
        dcol = sb("dcol", [P, 3])
        dn = sb("dn", [P, 2, 2])
        xT_hi = sb("xT_hi", [P, D], F32R)
        xT_lo = sb("xT_lo", [P, D], F32R)
        aggT_hi = sb("aggT_hi", [P, D], F32R)
        aggT_lo = sb("aggT_lo", [P, D], F32R)
        r0 = sb("r0", [P, D])
        x1 = sb("x1", [P, 2, D])
        gxT_hi = sb("gxT_hi", [P, D], F32R)
        gxT_lo = sb("gxT_lo", [P, D], F32R)
        h = sb("h", [P, DH])
        z = sb("z", [P, DH])
        gzT_hi = sb("gzT_hi", [P, DH], F32R)
        gzT_lo = sb("gzT_lo", [P, DH], F32R)
        bias_y = sb("bias_y", [P, D])
        base_y = sb("base_y", [P, D])
        r1 = sb("r1", [P, D])
        y_out = sb("y_out", [P, 2, D])
        st0 = sb("st0", [P, 6])
        st1 = sb("st1", [P, 6])
        sth = sb("sth", [P, HALVES, 6])
        mv0 = sb("mv0", [P, 2])
        mv1 = sb("mv1", [P, 2])
        mvh = sb("mvh", [P, 2])
        sd0 = sb("sd0", [P, 2])
        sd1 = sb("sd1", [P, 2])
        sdh = sb("sdh", [P, 2])
        nb1 = sb("nb1", [P, 1])
        nbh = sb("nbh", [P, 1])

        def bank(name):
            return ctx.enter_context(nc.psum_tensor(name, [P, BANK], F32))

        l0_ps = bank("l0_ps")
        h_ps = [bank("h_ps0"), bank("h_ps1")]
        y_ps = bank("y_ps")
        adj_ps = bank("adj_ps")
        xt_ps = bank("xt_ps")
        gz_ps = [bank("gz_ps0"), bank("gz_ps1")]

        w0_loaded, w1_loaded, w2_loaded = sem("w0_loaded"), sem("w1_loaded"), sem("w2_loaded")
        vec_loaded, bias_loaded = sem("vec_loaded"), sem("bias_loaded")
        consts = sem("consts")
        ident_made = sem("ident_made")
        vec_transposed, vec_copied, beta_widened = sem("vec_transposed"), sem("vec_copied"), sem("beta_widened")
        wT_ready, w_hi_done, w_lo_done = sem("wT_ready"), sem("w_hi_done"), sem("w_lo_done")
        w2_raw_done, v_ready, v_copied = sem("w2_raw_done"), sem("v_ready"), sem("v_copied")
        x_loaded = [sem("x_loaded0"), sem("x_loaded1")]
        adj_loaded = [sem("adj_loaded0"), sem("adj_loaded1")]
        stored = [sem("stored0"), sem("stored1")]
        deg_summed, deg_guarded, deg_inverted = sem("deg_summed"), sem("deg_guarded"), sem("deg_inverted")
        adj_normed = sem("adj_normed")
        adj_transposed, x_transposed = sem("adj_transposed"), sem("x_transposed")
        inc_made, count_guarded, count_inverted = sem("inc_made"), sem("count_guarded"), sem("count_inverted")
        adjT_done, inc_be_done, w_col_done = sem("adjT_done"), sem("inc_be_done"), sem("w_col_done")
        xT_hi_done, xT_lo_done = sem("xT_hi_done"), sem("xT_lo_done")
        agg_ready, aggT_hi_done, aggT_lo_done = sem("agg_ready"), sem("aggT_hi_done"), sem("aggT_lo_done")
        G_ready, G_done, dsum_done = sem("G_ready"), sem("G_done"), sem("dsum_done")
        d_guarded, d_positive, d_inverted, dn_done, dq_done = (
            sem("d_guarded"), sem("d_positive"), sem("d_inverted"), sem("dn_done"), sem("dq_done"))
        l0_ready, r0_done, st0_done, mv0_done, sd0_done, rs0_done, x1_done = (
            sem("l0_ready"), sem("r0_done"), sem("st0_done"), sem("mv0_done"), sem("sd0_done"),
            sem("rs0_done"), sem("x1_done"))
        gx_ready, gxT_hi_done, gxT_lo_done = sem("gx_ready"), sem("gxT_hi_done"), sem("gxT_lo_done")
        h_ready = [sem("h_ready0"), sem("h_ready1")]
        h_biased = [sem("h_biased0"), sem("h_biased1")]
        h_relued = [sem("h_relued0"), sem("h_relued1")]
        sth_done, mvh_done, sdh_done, rsh_done, nbh_done = (
            sem("sth_done"), sem("mvh_done"), sem("sdh_done"), sem("rsh_done"), sem("nbh_done"))
        z_done = sem("z_done")
        gz_ready = [sem("gz_ready0"), sem("gz_ready1")]
        gzT_hi_done = [sem("gzT_hi_done0"), sem("gzT_hi_done1")]
        gzT_lo_done = [sem("gzT_lo_done0"), sem("gzT_lo_done1")]
        bias_done, base_done = sem("bias_done"), sem("base_done")
        y_ready, r1_done, st1_done, mv1_done, sd1_done, rs1_done, nb1_done, y_done = (
            sem("y_ready"), sem("r1_done"), sem("st1_done"), sem("mv1_done"), sem("sd1_done"),
            sem("rs1_done"), sem("nb1_done"), sem("y_done"))

        w0_rows = stage_a[:, :].rearrange("p (o d) -> p o d", o=KD)
        w1_rows = stage_b[:, :].rearrange("p (o d) -> p o d", o=KH)
        w2_rows = stage_a[:, :].rearrange("p (o d) -> p o d", o=KD)
        w2_raw = stage_b[:, :].rearrange("p (k o) -> p k o", k=KH)
        groups = [(w0_rows, 0, k, w0_hi[:, k, :], w0_lo[:, k, :]) for k in range(K0)]
        groups += [(w1_rows, o, k, w1_hi[:, k, o * P:o * P + BANK], w1_lo[:, k, o * P:o * P + BANK])
                   for k in range(KD) for o in range(0, KH, 4)]
        groups += [(w2_rows, 0, k, w2_hi[:, k, :], w2_lo[:, k, :]) for k in range(KH)]
        W1_AT, W2_AT = K0, K0 + KD * HALVES
        group_ps = h_ps

        block = ctx.enter_context(nc.Block())

        @block.sync
        def _(sp):
            def load(g, p):
                if later(g, 2):
                    sp.wait_ge(r0_done, g - 1)
                    sp.wait_ge(agg_ready, g - 1)
                    sp.wait_ge(adj_transposed, g - 1)
                    sp.wait_ge(adj_normed, g - 1)
                sp.dma_start(adj_in[:, p, :], adj[g]).then_inc(adj_loaded[p], 16)
                sp.dma_start(x_in[:, p, :], x[g]).then_inc(x_loaded[p], 16)

            def store(g, p):
                sp.wait_ge(y_done, g + 1)
                sp.dma_start(out[g], y_out[:, p, :]).then_inc(stored[p], 16)

            sp.dma_start(stage_a[:, :].rearrange("p (o d) -> p o d", o=KD),
                         W0.rearrange("(o p) d -> p o d", p=P)).then_inc(w0_loaded, 16)
            sp.dma_start(stage_b[:, :].rearrange("p (o d) -> p o d", o=KH),
                         W1.rearrange("(o p) d -> p o d", p=P)).then_inc(w1_loaded, 16)
            load(0, 0)
            load(1, 1)
            sp.wait_ge(wT_ready, W1_AT)
            sp.dma_start(stage_a[:, :].rearrange("p (o d) -> p o d", o=KD),
                         W2.rearrange("(o p) d -> p o d", p=P)).then_inc(w2_loaded, 16)
            load(2, 0)
            for i in (0, 1):
                load(i + 3, (i + 1) % 2)
                store(i, i % 2)
            with sp.Fori(2, GRAPHS - 4, 2) as i:
                for e in range(2):
                    load(i + (e + 3), (e + 1) % 2)
                    store(i + e, e)
            for i in range(GRAPHS - 4, GRAPHS):
                if i + 3 < GRAPHS:
                    load(i + 3, (i + 1) % 2)
                store(i, i % 2)
            sp.wait_ge(stored[0], 8 * GRAPHS)
            sp.wait_ge(stored[1], 8 * GRAPHS)

        @block.gpsimd
        def _(pool):
            pool.dma_start(vec_rows[0:KH, :], gamma.rearrange("(k p) -> k p", p=P)).then_inc(vec_loaded, 16)
            pool.dma_start(vec_rows[KH:2 * KH, :], beta.rearrange("(k p) -> k p", p=P)).then_inc(vec_loaded, 16)
            pool.dma_start(b1_all[:, :], b1.rearrange("(a n) -> a n", a=1).to_broadcast([P, DH])).then_inc(
                bias_loaded, 16)
            pool.dma_start(b2_all[:, :], b2.rearrange("(a n) -> a n", a=1).to_broadcast([P, D])).then_inc(
                bias_loaded, 16)
            nc.gpsimd.memset(ident[:, :], 0.0).then_inc(consts, 1)
            nc.gpsimd.memset(ones[:, :], 1.0).then_inc(consts, 1)
            nc.gpsimd.memset(eps_col[:, :], LN_EPS).then_inc(consts, 1)
            nc.gpsimd.memset(incT_be[:, P + 1:P + 2], 1.0).then_inc(consts, 1)
            pool.wait_ge(consts, 4)
            nc.gpsimd.affine_select(out=ident[:, :], in_=ident[:, :], compare_op=ALU.not_equal, fill=1.0,
                                    base=0, pattern=[[-1, P]], channel_multiplier=1).then_inc(ident_made, 1)

        @block.tensor
        def _(pe):
            def three_passes(ps, parts, w_hi, w_lo, first, last):
                hi, lo = parts
                n = len(w_hi)
                for k in range(n):
                    nc.tensor.matmul(ps[:, :], hi[:, k * P:(k + 1) * P], w_hi[k], start=(first and k == 0), stop=False)
                    nc.tensor.matmul(ps[:, :], hi[:, k * P:(k + 1) * P], w_lo[k], start=False, stop=False)
                for k in range(n):
                    done = nc.tensor.matmul(ps[:, :], lo[:, k * P:(k + 1) * P], w_hi[k], start=False,
                                            stop=(last and k == n - 1))
                return done

            def transposes(g, p):
                pe.wait_ge(adj_loaded[p], half(g, p))
                pe.wait_ge(adj_normed, g + 1)
                if later(g, 1):
                    pe.wait_ge(G_done, g)
                    pe.wait_ge(dsum_done, g)
                nc.tensor.transpose(adj_ps[:, 0:P], adj_in[:, p, :], ident[:, :])
                nc.tensor.transpose(adj_ps[:, P:2 * P], adj_norm[:, :], ident[:, :]).then_inc(adj_transposed, 1)
                pe.wait_ge(x_loaded[p], half(g, p))
                if later(g, 2):
                    pe.wait_ge(gxT_lo_done, g - 1)
                if later(g, 1):
                    pe.wait_ge(xT_lo_done, g)
                for k in range(KD):
                    last = nc.tensor.transpose(xt_ps[:, k * P:(k + 1) * P], x_in[:, p, k * P:(k + 1) * P], ident[:, :])
                last.then_inc(x_transposed, 1)

            def aggregate_x(g, p):
                pe.wait_ge(adjT_done, g + 1)
                if later(g, 1):
                    pe.wait_ge(aggT_lo_done, g)
                if later(g, 2):
                    pe.wait_ge(gzT_lo_done[0], g - 1)
                for k in range(KD):
                    last = nc.tensor.matmul(gz_ps[0][:, k * P:(k + 1) * P], x_in[:, p, k * P:(k + 1) * P],
                                            adjT_norm[:, :], start=True, stop=True)
                last.then_inc(agg_ready, 1)
                pe.wait_ge(inc_be_done, g + 1)
                pe.wait_ge(w_col_done, g + 1)
                nc.tensor.matmul(adj_ps[:, 0:P + 2], incT[:, :], incT_be[:, :], start=True, stop=True).then_inc(
                    G_ready, 1)

            def layer0(g):
                pe.wait_ge(xT_hi_done, g + 1)
                pe.wait_ge(xT_lo_done, g + 1)
                if later(g, 1):
                    pe.wait_ge(r0_done, g)
                three_passes(l0_ps, (xT_hi, xT_lo), [w0_hi[:, k, :] for k in range(KD)],
                             [w0_lo[:, k, :] for k in range(KD)], True, False)
                pe.wait_ge(aggT_hi_done, g + 1)
                pe.wait_ge(aggT_lo_done, g + 1)
                three_passes(l0_ps, (aggT_hi, aggT_lo), [w0_hi[:, k, :] for k in range(KD, K0)],
                             [w0_lo[:, k, :] for k in range(KD, K0)], False, True).then_inc(l0_ready, 1)

            def aggregate_x1(g, p):
                pe.wait_ge(x1_done, g + 1)
                pe.wait_ge(G_done, g + 1)
                if not isinstance(g, int) or g + 1 < GRAPHS:
                    pe.wait_ge(xT_lo_done, g + 2)
                for k in range(KD):
                    last = nc.tensor.matmul(xt_ps[:, k * P:(k + 1) * P], x1[:, p, k * P:(k + 1) * P], G[:, p, :],
                                            start=True, stop=True)
                last.then_inc(gx_ready, 1)

            def layer1_w1(g):
                pe.wait_ge(gxT_hi_done, g + 1)
                pe.wait_ge(gxT_lo_done, g + 1)
                for n in range(HALVES):
                    if later(g, 1):
                        pe.wait_ge(h_biased[n], g)
                    cols = slice(n * BANK, (n + 1) * BANK)
                    three_passes(h_ps[n], (gxT_hi, gxT_lo), [w1_hi[:, k, cols] for k in range(KD)],
                                 [w1_lo[:, k, cols] for k in range(KD)], True, True).then_inc(h_ready[n], 1)

            def aggregate_z(g, p):
                for n in range(2):
                    pe.wait_ge(z_done, g * 2 + (n + 1))
                    if n == 0 and (not isinstance(g, int) or g + 1 < GRAPHS):
                        pe.wait_ge(aggT_lo_done, g + 2)
                    if later(g, 1):
                        pe.wait_ge(gzT_lo_done[n], g)
                    for k in range(KH // 2):
                        c = n * (KH // 2) + k
                        last = nc.tensor.matmul(gz_ps[n][:, k * P:(k + 1) * P], z[:, c * P:(c + 1) * P], G[:, p, :],
                                                start=True, stop=True)
                    last.then_inc(gz_ready[n], 1)

            def layer1_w2(g):
                if later(g, 1):
                    pe.wait_ge(r1_done, g)
                for n in range(2):
                    pe.wait_ge(gzT_hi_done[n], g + 1)
                    pe.wait_ge(gzT_lo_done[n], g + 1)
                    ks = range(n * KH // 2, (n + 1) * KH // 2)
                    cols = slice(n * BANK, (n + 1) * BANK)
                    done = three_passes(y_ps, (gzT_hi[:, cols], gzT_lo[:, cols]), [w2_hi[:, k, :] for k in ks],
                                        [w2_lo[:, k, :] for k in ks], n == 0, n == 1)
                done.then_inc(y_ready, 1)

            pe.wait_ge(ident_made, 1)
            pe.wait_ge(vec_loaded, 32)
            nc.tensor.transpose(adj_ps[:, 0:2 * KH], vec_rows[:, :], ident[0:2 * KH, 0:2 * KH]).then_inc(vec_transposed, 1)
            for n, (rows, o0, k, _, _) in enumerate(groups):
                for at, loaded in ((0, w0_loaded), (W1_AT, w1_loaded), (W2_AT, w2_loaded)):
                    if n == at:
                        pe.wait_ge(loaded, 16)
                if n >= 2:
                    pe.wait_ge(w_lo_done, n - 1)
                for o in range(4):
                    last = nc.tensor.transpose(group_ps[n % 2][:, o * P:(o + 1) * P],
                                               rows[:, o0 + o, k * P:(k + 1) * P], ident[:, :])
                last.then_inc(wT_ready, 1)
            pe.wait_ge(w2_raw_done, KH)
            pe.wait_ge(beta_widened, KH)
            for k in range(KH):
                last = nc.tensor.matmul(y_ps[:, :], beta_wide[:, k, :], w2_raw[:, k, :], start=(k == 0),
                                        stop=(k == KH - 1))
            last.then_inc(v_ready, 1)
            pe.wait_ge(w_lo_done, len(groups))
            pe.wait_ge(v_copied, 1)

            transposes(0, 0)
            aggregate_x(0, 0)
            layer0(0)
            transposes(1, 1)
            aggregate_x1(0, 0)
            aggregate_x(1, 1)
            layer1_w1(0)

            def iteration(i, e):
                layer0(i + 1)
                aggregate_z(i, e)
                transposes(i + 2, e)
                layer1_w2(i)
                aggregate_x1(i + 1, 1 - e)
                aggregate_x(i + 2, e)
                layer1_w1(i + 1)

            iteration(0, 0)
            iteration(1, 1)
            with pe.Fori(2, GRAPHS - 2, 2) as i:
                for e in range(2):
                    iteration(i + e if e else i, e)
            layer0(GRAPHS - 1)
            aggregate_z(GRAPHS - 2, 0)
            layer1_w2(GRAPHS - 2)
            aggregate_x1(GRAPHS - 1, 1)
            layer1_w1(GRAPHS - 1)
            aggregate_z(GRAPHS - 1, 1)
            layer1_w2(GRAPHS - 1)

        @block.scalar
        def _(act):
            def relu(g, n):
                act.wait_ge(h_biased[n], g + 1)
                c = slice(n * BANK, (n + 1) * BANK)
                nc.scalar.activation(h[:, c], h[:, c], ACT.Relu).then_inc(h_relued[n], 1)

            def normalise_h(g):
                act.wait_ge(mvh_done, g + 1)
                if later(g, 1):
                    act.wait_ge(nbh_done, g)
                nc.scalar.activation(sdh[:, 0:1], mvh[:, 1:2], ACT.Sqrt, bias=eps_col[:, :]).then_inc(sdh_done, 1)
                act.wait_ge(nbh_done, g + 1)
                for n in range(2):
                    if later(g, 1):
                        act.wait_ge(gz_ready[n], g)
                    c = slice(n * BANK, (n + 1) * BANK)
                    nc.scalar.activation(z[:, c], h[:, c], ACT.Identity, bias=nbh[:, :], scale=sdh[:, 1:2]).then_inc(
                        z_done, 1)

            def gzT_high(g):
                for n in range(2):
                    act.wait_ge(gz_ready[n], g + 1)
                    if later(g, 1):
                        act.wait_ge(y_ready, g)
                    c = slice(n * BANK, (n + 1) * BANK)
                    nc.scalar.activation(gzT_hi[:, c], gz_ps[n][:, :], ACT.Identity).then_inc(gzT_hi_done[n], 1)

            def root0(g):
                act.wait_ge(mv0_done, g + 1)
                nc.scalar.activation(sd0[:, 0:1], mv0[:, 1:2], ACT.Sqrt, bias=eps_col[:, :]).then_inc(sd0_done, 1)

            def xT_high(g):
                act.wait_ge(x_transposed, g + 1)
                if later(g, 1):
                    act.wait_ge(l0_ready, g)
                nc.scalar.activation(xT_hi[:, :], xt_ps[:, :], ACT.Identity).then_inc(xT_hi_done, 1)

            def gxT_high(g):
                act.wait_ge(gx_ready, g + 1)
                if later(g, 1):
                    act.wait_ge(h_ready[1], g)
                nc.scalar.activation(gxT_hi[:, :], xt_ps[:, :], ACT.Identity).then_inc(gxT_hi_done, 1)

            def aggT_high(g):
                act.wait_ge(agg_ready, g + 1)
                if later(g, 1):
                    act.wait_ge(l0_ready, g)
                nc.scalar.activation(aggT_hi[:, :], gz_ps[0][:, :], ACT.Identity).then_inc(aggT_hi_done, 1)

            def root1(g):
                act.wait_ge(mv1_done, g + 1)
                nc.scalar.activation(sd1[:, 0:1], mv1[:, 1:2], ACT.Sqrt, bias=eps_col[:, :]).then_inc(sd1_done, 1)

            def normalise_out(g, p):
                act.wait_ge(nb1_done, g + 1)
                if later(g, 2):
                    act.wait_ge(stored[p], half(g, p) - 16)
                nc.scalar.activation(y_out[:, p, :], r1[:, :], ACT.Identity, bias=nb1[:, :], scale=sd1[:, 1:2]).then_inc(
                    y_done, 1)

            act.wait_ge(consts, 3)
            for n, (_, _, k, hi, _) in enumerate(groups):
                act.wait_ge(wT_ready, n + 1)
                if n >= W2_AT:
                    if n == W2_AT:
                        act.wait_ge(vec_copied, 1)
                    nc.scalar.activation(hi, group_ps[n % 2][:, :], ACT.Identity,
                                         scale=vec_cols[:, k:k + 1]).then_inc(w_hi_done, 1)
                else:
                    nc.scalar.activation(hi, group_ps[n % 2][:, :], ACT.Identity).then_inc(w_hi_done, 1)

            xT_high(0)
            aggT_high(0)
            root0(0)
            xT_high(1)
            gxT_high(0)
            aggT_high(1)
            relu(0, 0)

            def iteration(i, e):
                relu(i, 1)
                normalise_h(i)
                gzT_high(i)
                root0(i + 1)
                xT_high(i + 2)
                gxT_high(i + 1)
                root1(i)
                aggT_high(i + 2)
                normalise_out(i, e)
                relu(i + 1, 0)

            iteration(0, 0)
            iteration(1, 1)
            with act.Fori(2, GRAPHS - 2, 2) as i:
                for e in range(2):
                    iteration(i + e if e else i, e)
            i = GRAPHS - 2
            relu(i, 1)
            normalise_h(i)
            gzT_high(i)
            root0(i + 1)
            gxT_high(i + 1)
            root1(i)
            normalise_out(i, 0)
            relu(i + 1, 0)
            relu(i + 1, 1)
            normalise_h(i + 1)
            gzT_high(i + 1)
            root1(i + 1)
            normalise_out(i + 1, 1)

        @block.vector
        def _(dve):
            def normalise_adj(g, p, h_stats=None):
                dve.wait_ge(adj_loaded[p], half(g, p))
                if h_stats is not None:
                    dve.wait_ge(sth_done, h_stats * 2 + 2)
                nc.vector.reduce_sum(deg[:, 0:1], adj_in[:, p, :], axis=AX_X).then_inc(deg_summed, 1)
                if h_stats is not None:
                    aggregate_h()
                dve.wait_ge(deg_summed, g + 1)
                nc.vector.tensor_scalar_max(deg[:, 1:2], deg[:, 0:1], DEG_EPS).then_inc(deg_guarded, 1)
                dve.wait_ge(deg_guarded, g + 1)
                nc.vector.reciprocal(deg[:, 2:3], deg[:, 1:2]).then_inc(deg_inverted, 1)
                dve.wait_ge(deg_inverted, g + 1)
                if later(g, 1):
                    dve.wait_ge(adj_transposed, g)
                nc.vector.tensor_scalar_mul(adj_norm[:, :], adj_in[:, p, :], deg[:, 2:3]).then_inc(adj_normed, 1)

            def incidence(g, stats0=None):
                dve.wait_ge(adj_transposed, g + 1)
                if later(g, 1):
                    dve.wait_ge(agg_ready, g)
                    dve.wait_ge(G_ready, g)
                if stats0 is not None:
                    dve.wait_ge(st0_done, stats0 + 1)
                nc.vector.tensor_scalar(incT[:, :], adj_ps[:, 0:P], 0.0, 0.0, ALU.not_equal, ALU.add,
                                        accum_out=count[:, 0:1]).then_inc(inc_made, 1)
                if stats0 is not None:
                    aggregate0()
                nc.vector.tensor_copy(adjT_norm[:, :], adj_ps[:, P:2 * P]).then_inc(adjT_done, 1)
                nc.vector.tensor_copy(incT_be[:, P:P + 1], adj_ps[:, 0:1]).then_inc(w_col_done, 1)
                dve.wait_ge(inc_made, g + 1)
                nc.vector.tensor_scalar_max(count[:, 1:2], count[:, 0:1], 1.0).then_inc(count_guarded, 1)
                dve.wait_ge(count_guarded, g + 1)
                nc.vector.reciprocal(count[:, 2:3], count[:, 1:2]).then_inc(count_inverted, 1)
                dve.wait_ge(count_inverted, g + 1)
                nc.vector.tensor_scalar_mul(incT_be[:, 0:P], incT[:, :], count[:, 2:3]).then_inc(inc_be_done, 1)

            def copy_G(g, p):
                dve.wait_ge(G_ready, g + 1)
                if later(g, 2):
                    dve.wait_ge(gz_ready[1], g - 1)
                nc.vector.tensor_copy(G[:, p, :], adj_ps[:, 0:P]).then_inc(G_done, 1)
                nc.vector.tensor_copy(dsum[:, :], adj_ps[:, P:P + 2]).then_inc(dsum_done, 1)
                dve.wait_ge(dsum_done, g + 1)
                nc.vector.tensor_scalar_max(dcol[:, 0:1], dsum[:, 0:1], TINY).then_inc(d_guarded, 1)
                nc.vector.tensor_single_scalar(dcol[:, 1:2], dsum[:, 0:1], 0.0, ALU.is_gt).then_inc(d_positive, 1)
                dve.wait_ge(d_guarded, g + 1)
                nc.vector.reciprocal(dcol[:, 2:3], dcol[:, 0:1]).then_inc(d_inverted, 1)
                dve.wait_ge(d_positive, g + 1)
                dve.wait_ge(d_inverted, g + 1)
                nc.vector.tensor_tensor(dn[:, p, 0:1], dcol[:, 1:2], dcol[:, 2:3], ALU.mult).then_inc(dn_done, 1)
                dve.wait_ge(dn_done, g + 1)
                nc.vector.tensor_tensor(dn[:, p, 1:2], dn[:, p, 0:1], dsum[:, 1:2], ALU.mult).then_inc(dq_done, 1)

            def xT_low(g):
                dve.wait_ge(xT_hi_done, g + 1)
                nc.vector.tensor_tensor(xT_lo[:, :], xt_ps[:, :], xT_hi[:, :].bitcast(F32), ALU.subtract).then_inc(
                    xT_lo_done, 1)

            def aggT_low(g):
                dve.wait_ge(aggT_hi_done, g + 1)
                nc.vector.tensor_tensor(aggT_lo[:, :], gz_ps[0][:, :], aggT_hi[:, :].bitcast(F32),
                                        ALU.subtract).then_inc(aggT_lo_done, 1)

            def gxT_low(g, stats1=None):
                dve.wait_ge(gxT_hi_done, g + 1)
                if stats1 is not None:
                    dve.wait_ge(st1_done, stats1 + 1)
                nc.vector.tensor_tensor(gxT_lo[:, :], xt_ps[:, :], gxT_hi[:, :].bitcast(F32),
                                        ALU.subtract).then_inc(gxT_lo_done, 1)
                if stats1 is not None:
                    aggregate1()

            def gzT_low(g):
                for n in range(2):
                    dve.wait_ge(gzT_hi_done[n], g + 1)
                    c = slice(n * BANK, (n + 1) * BANK)
                    nc.vector.tensor_tensor(gzT_lo[:, c], gz_ps[n][:, :], gzT_hi[:, c].bitcast(F32),
                                            ALU.subtract).then_inc(gzT_lo_done[n], 1)

            def residual0(g, p):
                dve.wait_ge(l0_ready, g + 1)
                if later(g, 1):
                    dve.wait_ge(x1_done, g)
                nc.vector.scalar_tensor_tensor(out=r0[:, :], in0=l0_ps[:, :], scalar=0.0, in1=x_in[:, p, :],
                                               op0=ALU.max, op1=ALU.add).then_inc(r0_done, 1)
                dve.wait_ge(r0_done, g + 1)
                nc.vector.bn_stats(st0[:, :], r0[:, :]).then_inc(st0_done, 1)

            def aggregate0():
                nc.vector.bn_aggr(mv0[:, :], st0[:, :]).then_inc(mv0_done, 1)

            def normalise_x1(g, p):
                dve.wait_ge(sd0_done, g + 1)
                nc.vector.reciprocal(sd0[:, 1:2], sd0[:, 0:1]).then_inc(rs0_done, 1)
                dve.wait_ge(rs0_done, g + 1)
                if later(g, 2):
                    dve.wait_ge(base_done, g - 1)
                    dve.wait_ge(gx_ready, g - 1)
                nc.vector.tensor_scalar(x1[:, p, :], r0[:, :], mv0[:, 0:1], sd0[:, 1:2], ALU.subtract,
                                        ALU.mult).then_inc(x1_done, 1)

            def bias_h(g, p, n):
                dve.wait_ge(h_ready[n], g + 1)
                dve.wait_ge(dn_done, g + 1)
                if later(g, 1):
                    dve.wait_ge(z_done, g * 2)
                c = slice(n * BANK, (n + 1) * BANK)
                nc.vector.scalar_tensor_tensor(out=h[:, c], in0=h_ps[n][:, :], scalar=dn[:, p, 0:1], in1=b1_all[:, c],
                                               op0=ALU.mult, op1=ALU.add).then_inc(h_biased[n], 1)

            def stats_h(g, n):
                dve.wait_ge(h_relued[n], g + 1)
                nc.vector.bn_stats(sth[:, n, :], h[:, n * BANK:(n + 1) * BANK]).then_inc(sth_done, 1)

            def aggregate_h():
                nc.vector.bn_aggr(mvh[:, :], sth[:, :, :].rearrange("p a b -> p (a b)")).then_inc(mvh_done, 1)

            def scales_h(g):
                dve.wait_ge(sdh_done, g + 1)
                nc.vector.reciprocal(sdh[:, 1:2], sdh[:, 0:1]).then_inc(rsh_done, 1)
                dve.wait_ge(rsh_done, g + 1)
                nc.vector.scalar_tensor_tensor(out=nbh[:, :], in0=mvh[:, 0:1], scalar=-1.0, in1=sdh[:, 1:2],
                                               op0=ALU.mult, op1=ALU.mult).then_inc(nbh_done, 1)

            def base(g, p):
                dve.wait_ge(dq_done, g + 1)
                if later(g, 1):
                    dve.wait_ge(base_done, g)
                nc.vector.scalar_tensor_tensor(out=bias_y[:, :], in0=v_all[:, :], scalar=dn[:, p, 1:2], in1=b2_all[:, :],
                                               op0=ALU.mult, op1=ALU.add).then_inc(bias_done, 1)
                dve.wait_ge(bias_done, g + 1)
                dve.wait_ge(x1_done, g + 1)
                if later(g, 1):
                    dve.wait_ge(r1_done, g)
                nc.vector.scalar_tensor_tensor(out=base_y[:, :], in0=x1[:, p, :], scalar=2.0, in1=bias_y[:, :],
                                               op0=ALU.mult, op1=ALU.add).then_inc(base_done, 1)

            def residual1(g, p):
                dve.wait_ge(y_ready, g + 1)
                dve.wait_ge(base_done, g + 1)
                if later(g, 1):
                    dve.wait_ge(y_done, g)
                nc.vector.scalar_tensor_tensor(out=r1[:, :], in0=y_ps[:, :], scalar=dn[:, p, 0:1], in1=base_y[:, :],
                                               op0=ALU.mult, op1=ALU.add).then_inc(r1_done, 1)
                dve.wait_ge(r1_done, g + 1)
                nc.vector.bn_stats(st1[:, :], r1[:, :]).then_inc(st1_done, 1)

            def aggregate1():
                nc.vector.bn_aggr(mv1[:, :], st1[:, :]).then_inc(mv1_done, 1)

            def scales1(g):
                dve.wait_ge(sd1_done, g + 1)
                nc.vector.reciprocal(sd1[:, 1:2], sd1[:, 0:1]).then_inc(rs1_done, 1)
                dve.wait_ge(rs1_done, g + 1)
                nc.vector.scalar_tensor_tensor(out=nb1[:, :], in0=mv1[:, 0:1], scalar=-1.0, in1=sd1[:, 1:2],
                                               op0=ALU.mult, op1=ALU.mult).then_inc(nb1_done, 1)

            dve.wait_ge(vec_transposed, 1)
            nc.vector.tensor_copy(vec_cols[:, :], adj_ps[:, 0:2 * KH]).then_inc(vec_copied, 1)
            dve.wait_ge(vec_copied, 1)
            dve.wait_ge(consts, 4)
            for k in range(KH):
                nc.vector.tensor_scalar_mul(beta_wide[:, k, :], ones[:, :], vec_cols[:, KH + k:KH + k + 1]).then_inc(
                    beta_widened, 1)
            for n, (_, _, k, hi, lo) in enumerate(groups):
                dve.wait_ge(w_hi_done, n + 1)
                if n >= W2_AT:
                    if n == W2_AT:
                        dve.wait_ge(wT_ready, W2_AT)
                    nc.vector.tensor_copy(w2_raw[:, k, :], group_ps[n % 2][:, :]).then_inc(w2_raw_done, 1)
                    nc.vector.scalar_tensor_tensor(out=lo, in0=group_ps[n % 2][:, :], scalar=vec_cols[:, k:k + 1],
                                                   in1=hi.bitcast(F32), op0=ALU.mult, op1=ALU.subtract).then_inc(
                        w_lo_done, 1)
                else:
                    nc.vector.tensor_tensor(lo, group_ps[n % 2][:, :], hi.bitcast(F32), ALU.subtract).then_inc(
                        w_lo_done, 1)
            dve.wait_ge(v_ready, 1)
            nc.vector.tensor_copy(v_all[:, :], y_ps[:, :]).then_inc(v_copied, 1)
            dve.wait_ge(v_copied, 1)
            dve.wait_ge(bias_loaded, 32)

            normalise_adj(0, 0)
            incidence(0)
            xT_low(0)
            aggT_low(0)
            copy_G(0, 0)
            normalise_adj(1, 1)
            residual0(0, 0)
            incidence(1, stats0=0)
            normalise_x1(0, 0)
            xT_low(1)
            gxT_low(0)
            aggT_low(1)
            copy_G(1, 1)
            bias_h(0, 0, 0)
            stats_h(0, 0)

            def iteration(i, e):
                bias_h(i, e, 1)
                stats_h(i, 1)
                normalise_adj(i + 2, e, h_stats=i)
                scales_h(i)
                base(i, e)
                gzT_low(i)
                residual0(i + 1, 1 - e)
                incidence(i + 2, stats0=i + 1)
                normalise_x1(i + 1, 1 - e)
                xT_low(i + 2)
                residual1(i, e)
                gxT_low(i + 1, stats1=i)
                scales1(i)
                aggT_low(i + 2)
                copy_G(i + 2, e)
                bias_h(i + 1, 1 - e, 0)
                stats_h(i + 1, 0)

            iteration(0, 0)
            iteration(1, 1)
            with dve.Fori(2, GRAPHS - 2, 2) as i:
                for e in range(2):
                    iteration(i + e if e else i, e)
            i = GRAPHS - 2
            bias_h(i, 0, 1)
            stats_h(i, 1)
            dve.wait_ge(sth_done, 2 * i + 2)
            aggregate_h()
            scales_h(i)
            base(i, 0)
            gzT_low(i)
            residual0(i + 1, 1)
            dve.wait_ge(st0_done, i + 2)
            aggregate0()
            normalise_x1(i + 1, 1)
            residual1(i, 0)
            gxT_low(i + 1, stats1=i)
            scales1(i)
            for n in range(2):
                bias_h(i + 1, 1, n)
                stats_h(i + 1, n)
            dve.wait_ge(sth_done, 2 * i + 4)
            aggregate_h()
            scales_h(i + 1)
            base(i + 1, 1)
            gzT_low(i + 1)
            residual1(i + 1, 1)
            dve.wait_ge(st1_done, i + 2)
            aggregate1()
            scales1(i + 1)


_INS = ["x", "adj", "L0_gnn_W", "L1_gnn_W1", "L1_gnn_b1", "L1_gnn_gamma", "L1_gnn_beta", "L1_gnn_W2", "L1_gnn_b2"]


def kernel(**inputs):
    import numpy as np
    import concourse.bacc as bacc
    from concourse.bass_utils import run_bass_kernel_spmd

    nc = bacc.Bacc("TRN2", target_bir_lowering=False, num_devices=1)
    arrays, args = {}, []
    for name in _INS:
        a = np.ascontiguousarray(inputs[name])
        arrays[f"in_{name}"] = a
        args.append(nc.dram_tensor(f"in_{name}", a.shape, mybir.dt.from_np(a.dtype), kind="ExternalInput").ap())
    out = nc.dram_tensor("out_0", inputs["x"].shape, F32, kind="ExternalOutput").ap()
    two_layer_graph_kernel(nc, *args, out)
    r = run_bass_kernel_spmd(nc, [arrays], core_ids=[0])
    return r.results[0]["out_0"]
```

```python
from contextlib import ExitStack

import concourse.bass as bass
from concourse import mybir

P = 128
BANK = 512

ALU = mybir.AluOpType
ACT = mybir.ActivationFunctionType
F32 = mybir.dt.float32
F32R = mybir.dt.float32r
F16 = mybir.dt.float16
AX_X = mybir.AxisListType.X

DEG_EPS = 1e-6
LN_EPS = 1e-5
PART_SCALE = 256.0
TINY = 1.1754944e-38


def later(g, n):
    return not isinstance(g, int) or g >= n


def within(g, graphs):
    return not isinstance(g, int) or g < graphs


def loads(g, p):
    return (g - p) * 8 + 16


def two_layer_graph_kernel(nc, x, adj, W0, W1, b1, gamma, beta, W2, b2, out):
    GRAPHS, NODES, D = x.shape
    DH = W1.shape[0]
    KD = D // P
    KH = DH // P
    K0 = 2 * KD
    HALVES = DH // BANK
    ADJ_AHEAD, X_AHEAD = 4, 3
    assert NODES == P and D == BANK and DH == 2 * BANK and GRAPHS % 2 == 0 and GRAPHS >= 8

    with ExitStack() as ctx:
        def sb(name, shape, dt=F32):
            return ctx.enter_context(nc.sbuf_tensor(name, shape, dt))

        def sem(name):
            return ctx.enter_context(nc.semaphore(name))

        w0_hi = sb("w0_hi", [P, K0, D], F32R)
        w0_lo = sb("w0_lo", [P, K0, D], F32R)
        w1_hi = sb("w1_hi", [P, KD, DH], F32R)
        w1_lo = sb("w1_lo", [P, KD, DH], F32R)
        w2_hi = sb("w2_hi", [P, KH, D], F32R)
        w2_lo = sb("w2_lo", [P, KH, D], F32R)
        stage_a = sb("stage_a", [P, 4 * 1024])
        stage_b = sb("stage_b", [P, 4 * 1024])
        gamma_rows = sb("gamma_rows", [KH, P])
        gamma_cols = sb("gamma_cols", [P, KH])
        beta_all = sb("beta_all", [P, DH])
        v_cols = sb("v_cols", [P, KD])
        v_diag = sb("v_diag", [P, KD, P])
        ident = sb("ident", [P, P])
        ones = sb("ones", [P, P])
        eps_col = sb("eps_col", [P, 1])
        root_warm = sb("root_warm", [P, 1])
        eps_scaled = sb("eps_scaled", [P, 1])
        b1_all = sb("b1_all", [P, DH])
        b2_all = sb("b2_all", [P, D])
        v_all = sb("v_all", [P, D])

        x_in = sb("x_in", [P, 2, D])
        adj_in = sb("adj_in", [P, 2, P])
        adj_norm = sb("adj_norm", [P, P])
        deg = sb("deg", [P, 3])
        adjT_norm = sb("adjT_norm", [P, P])
        incT = sb("incT", [P, P])
        count = sb("count", [P, 3])
        incT_be = sb("incT_be", [P, P + 2])
        G_hi = sb("G_hi", [P, 2, P], F16)
        G_lo = sb("G_lo", [P, 2, P], F16)
        dsum = sb("dsum", [P, 2])
        dcol = sb("dcol", [P, 3])
        dn = sb("dn", [P, 2, 2])
        xT_hi = sb("xT_hi", [P, D], F32R)
        xT_lo = sb("xT_lo", [P, D], F32R)
        aggT_hi = sb("aggT_hi", [P, D], F32R)
        aggT_lo = sb("aggT_lo", [P, D], F32R)
        r0 = sb("r0", [P, D])
        x1 = sb("x1", [P, 2, D])
        x1_hi = sb("x1_hi", [P, D], F16)
        x1_lo = sb("x1_lo", [P, D], F16)
        gxT_hi = sb("gxT_hi", [P, D], F32R)
        gxT_lo = sb("gxT_lo", [P, D], F32R)
        h = sb("h", [P, DH])
        z = sb("z", [P, DH])
        z_hi = sb("z_hi", [P, DH], F16)
        z_lo = sb("z_lo", [P, DH], F16)
        gzT_hi = sb("gzT_hi", [P, DH], F32R)
        gzT_lo = sb("gzT_lo", [P, DH], F32R)
        bias_y = sb("bias_y", [P, D])
        base_y = sb("base_y", [P, D])
        r1 = sb("r1", [P, D])
        y_out = sb("y_out", [P, 2, D])
        st0 = sb("st0", [P, 6])
        st1 = sb("st1", [P, 6])
        sth = sb("sth", [P, HALVES, 6])
        mv0 = sb("mv0", [P, 2])
        mv1 = sb("mv1", [P, 2])
        mvh = sb("mvh", [P, 2])
        sd0 = sb("sd0", [P, 2])
        sd1 = sb("sd1", [P, 2])
        sdh = sb("sdh", [P, 2])
        nb1 = sb("nb1", [P, 1])
        nbh = sb("nbh", [P, 1])

        def bank(name):
            return ctx.enter_context(nc.psum_tensor(name, [P, BANK], F32))

        l0_ps = bank("l0_ps")
        h_ps = [bank("h_ps0"), bank("h_ps1")]
        y_ps = bank("y_ps")
        adj_ps = bank("adj_ps")
        gx_ps = bank("gx_ps")
        gz_ps = [bank("gz_ps0"), bank("gz_ps1")]
        agg_ps, xt_ps = h_ps[0], gx_ps

        w0_loaded = [sem("w0_loaded0"), sem("w0_loaded1")]
        w1_loaded = [sem("w1_loaded0"), sem("w1_loaded1")]
        w2_loaded = [sem("w2_loaded0"), sem("w2_loaded1")]
        gamma_loaded, beta_loaded, bias_loaded = sem("gamma_loaded"), sem("beta_loaded"), sem("bias_loaded")
        consts, ident_made = sem("consts"), sem("ident_made")
        gamma_transposed, gamma_copied = sem("gamma_transposed"), sem("gamma_copied")
        wT_ready, w_hi_done, w_lo_done = sem("wT_ready"), sem("w_hi_done"), sem("w_lo_done")
        v_product_done = sem("v_product_done")
        v_summed, v_spread, v_ready, v_copied = sem("v_summed"), sem("v_spread"), sem("v_ready"), sem("v_copied")
        x_loaded = [sem("x_loaded0"), sem("x_loaded1")]
        adj_loaded = [sem("adj_loaded0"), sem("adj_loaded1")]
        stored = [sem("stored0"), sem("stored1")]
        deg_summed, deg_guarded, deg_inverted = sem("deg_summed"), sem("deg_guarded"), sem("deg_inverted")
        adj_normed = sem("adj_normed")
        adj_transposed, x_transposed = sem("adj_transposed"), sem("x_transposed")
        inc_made, count_guarded, count_inverted = sem("inc_made"), sem("count_guarded"), sem("count_inverted")
        adjT_done, inc_be_done, w_col_done = sem("adjT_done"), sem("inc_be_done"), sem("w_col_done")
        xT_hi_done, xT_lo_done = sem("xT_hi_done"), sem("xT_lo_done")
        agg_ready, aggT_hi_done, aggT_lo_done = sem("agg_ready"), sem("aggT_hi_done"), sem("aggT_lo_done")
        G_ready, G_hi_done, G_lo_done, dsum_done = (
            sem("G_ready"), sem("G_hi_done"), sem("G_lo_done"), sem("dsum_done"))
        d_guarded, d_positive, d_inverted, dn_done, dq_done = (
            sem("d_guarded"), sem("d_positive"), sem("d_inverted"), sem("dn_done"), sem("dq_done"))
        l0_ready, r0_done, st0_done, mv0_done, sd0_done, rs0_done, x1_done = (
            sem("l0_ready"), sem("r0_done"), sem("st0_done"), sem("mv0_done"), sem("sd0_done"),
            sem("rs0_done"), sem("x1_done"))
        x1_hi_done, x1_lo_done = sem("x1_hi_done"), sem("x1_lo_done")
        gx_ready, gxT_hi_done, gxT_lo_done = sem("gx_ready"), sem("gxT_hi_done"), sem("gxT_lo_done")
        h_ready = [sem("h_ready0"), sem("h_ready1")]
        h_biased = [sem("h_biased0"), sem("h_biased1")]
        h_relued = [sem("h_relued0"), sem("h_relued1")]
        sth_done, mvh_done, sdh_done, rsh_done, nbh_done = (
            sem("sth_done"), sem("mvh_done"), sem("sdh_done"), sem("rsh_done"), sem("nbh_done"))
        z_done, z_hi_done, z_lo_done = sem("z_done"), sem("z_hi_done"), sem("z_lo_done")
        gz_ready = [sem("gz_ready0"), sem("gz_ready1")]
        gzT_hi_done = [sem("gzT_hi_done0"), sem("gzT_hi_done1")]
        gzT_lo_done = [sem("gzT_lo_done0"), sem("gzT_lo_done1")]
        bias_done, base_done = sem("bias_done"), sem("base_done")
        y_ready, r1_done, st1_done, mv1_done, sd1_done, rs1_done, nb1_done, y_done = (
            sem("y_ready"), sem("r1_done"), sem("st1_done"), sem("mv1_done"), sem("sd1_done"),
            sem("rs1_done"), sem("nb1_done"), sem("y_done"))

        w0_rows = stage_a[:, :].rearrange("p (o d) -> p o d", o=KD)
        w1_rows = stage_b[:, :].rearrange("p (o d) -> p o d", o=KH)
        w2_rows = stage_a[:, :].rearrange("p (o d) -> p o d", o=KD)
        groups = [(w0_rows, 0, k, w0_hi[:, k, :], w0_lo[:, k, :]) for k in range(K0)]
        groups += [(w1_rows, o, k, w1_hi[:, k, o * P:o * P + BANK], w1_lo[:, k, o * P:o * P + BANK])
                   for o in range(0, KH, 4) for k in range(KD)]
        groups += [(w2_rows, 0, k, w2_hi[:, k, :], w2_lo[:, k, :]) for k in range(KH)]
        W1_AT, W2_AT = K0, K0 + KD * HALVES
        group_ps = [y_ps, gz_ps[0], h_ps[1]]
        TURNS = len(group_ps)
        group_loaded = {0: w0_loaded[0], K0 // 2: w0_loaded[1], W1_AT: w1_loaded[0], W1_AT + KD: w1_loaded[1],
                        W2_AT: w2_loaded[0], W2_AT + KH // 2: w2_loaded[1]}

        block = ctx.enter_context(nc.Block())

        @block.sync
        def _(sp):
            def load_adj(g, p):
                if later(g, 2):
                    sp.wait_ge(adj_transposed, g - 1)
                    sp.wait_ge(adj_normed, g - 1)
                sp.dma_start(adj_in[:, p, :], adj[g]).then_inc(adj_loaded[p], 16)

            def load_x(g, p):
                if later(g, 2):
                    sp.wait_ge(r0_done, g - 1)
                    sp.wait_ge(agg_ready, g - 1)
                    sp.wait_ge(x_transposed, g - 1)
                sp.dma_start(x_in[:, p, :], x[g]).then_inc(x_loaded[p], 16)

            def store(g, p):
                sp.wait_ge(y_done, g + 1)
                sp.dma_start(out[g], y_out[:, p, :]).then_inc(stored[p], 16)

            def iteration(i, e):
                if within(i + ADJ_AHEAD, GRAPHS):
                    load_adj(i + ADJ_AHEAD, e)
                if within(i + X_AHEAD, GRAPHS):
                    load_x(i + X_AHEAD, 1 - e)
                store(i, e)

            load_adj(0, 0)
            load_x(0, 0)
            w0_dram = W0.rearrange("(o p) d -> p o d", p=P)
            w1_dram = W1.rearrange("(o p) d -> p o d", p=P)
            w2_dram = W2.rearrange("(o p) d -> p o d", p=P)
            for n in range(2):
                c = slice(n * BANK, (n + 1) * BANK)
                sp.dma_start(w0_rows[:, :, c], w0_dram[:, :, c]).then_inc(w0_loaded[n], 16)
                if n == 0:
                    load_adj(1, 1)
            for n in range(2):
                o = slice(n * KH // 2, (n + 1) * KH // 2)
                sp.dma_start(w1_rows[:, o, :], w1_dram[:, o, :]).then_inc(w1_loaded[n], 16)
            load_x(1, 1)
            for n in range(2):
                sp.wait_ge(wT_ready, (n + 1) * K0 // 2)
                c = slice(n * BANK, (n + 1) * BANK)
                sp.dma_start(w2_rows[:, :, c], w2_dram[:, :, c]).then_inc(w2_loaded[n], 16)
            load_adj(2, 0)
            load_adj(3, 1)
            load_x(2, 0)
            iteration(0, 0)
            iteration(1, 1)
            with sp.Fori(2, GRAPHS - ADJ_AHEAD - 2, 2) as i:
                for e in range(2):
                    iteration(i + e if e else i, e)
            for i in range(GRAPHS - ADJ_AHEAD - 2, GRAPHS):
                iteration(i, i % 2)
            sp.wait_ge(stored[0], 8 * GRAPHS)
            sp.wait_ge(stored[1], 8 * GRAPHS)

        @block.gpsimd
        def _(pool):
            nc.gpsimd.memset(ident[:, :], 0.0).then_inc(consts, 1)
            nc.gpsimd.memset(ones[:, :], 1.0).then_inc(consts, 1)
            nc.gpsimd.memset(eps_col[:, :], LN_EPS).then_inc(consts, 1)
            nc.gpsimd.memset(eps_scaled[:, :], LN_EPS / PART_SCALE ** 2).then_inc(consts, 1)
            nc.gpsimd.memset(incT_be[:, P + 1:P + 2], 1.0).then_inc(consts, 1)
            pool.wait_ge(consts, 5)
            nc.gpsimd.affine_select(out=ident[:, :], in_=ident[:, :], compare_op=ALU.not_equal, fill=1.0,
                                    base=0, pattern=[[-1, P]], channel_multiplier=1).then_inc(ident_made, 1)
            pool.dma_start(gamma_rows[:, :], gamma.rearrange("(k p) -> k p", p=P)).then_inc(gamma_loaded, 16)
            pool.dma_start(beta_all[:, :], beta.rearrange("(a n) -> a n", a=1).to_broadcast([P, DH])).then_inc(
                beta_loaded, 16)
            pool.wait_ge(beta_loaded, 16)
            pool.wait_ge(w2_loaded[0], 16)
            pool.wait_ge(w2_loaded[1], 16)
            pool.dma_start(b1_all[:, :], b1.rearrange("(a n) -> a n", a=1).to_broadcast([P, DH])).then_inc(
                bias_loaded, 16)
            pool.dma_start(b2_all[:, :], b2.rearrange("(a n) -> a n", a=1).to_broadcast([P, D])).then_inc(
                bias_loaded, 16)
            pool.wait_ge(wT_ready, W2_AT)
            for k in range(KD):
                nc.gpsimd.tensor_tensor(stage_b[:, k * DH:(k + 1) * DH], w2_rows[:, k, :], beta_all[:, :],
                                        ALU.mult).then_inc(v_product_done, 1)

        @block.tensor
        def _(pe):
            def hi_passes(ps, hi, w_hi, w_lo, first):
                for k in range(len(w_hi)):
                    nc.tensor.matmul(ps[:, :], hi[:, k * P:(k + 1) * P], w_hi[k], start=(first and k == 0), stop=False)
                    nc.tensor.matmul(ps[:, :], hi[:, k * P:(k + 1) * P], w_lo[k], start=False, stop=False)

            def lo_passes(ps, lo, w_hi, last):
                for k in range(len(w_hi)):
                    done = nc.tensor.matmul(ps[:, :], lo[:, k * P:(k + 1) * P], w_hi[k], start=False,
                                            stop=(last and k == len(w_hi) - 1))
                return done

            def by_G(ps, hi, lo, p):
                for k in range(BANK // P):
                    c = slice(k * P, (k + 1) * P)
                    nc.tensor.matmul(ps[:, c], hi[:, c], G_hi[:, p, :], start=True, stop=False)
                    nc.tensor.matmul(ps[:, c], hi[:, c], G_lo[:, p, :], start=False, stop=False)
                    done = nc.tensor.matmul(ps[:, c], lo[:, c], G_hi[:, p, :], start=False, stop=True)
                return done

            def transpose_adj(g, p):
                pe.wait_ge(adj_loaded[p], loads(g, p))
                if later(g, 1):
                    pe.wait_ge(G_lo_done, g)
                    pe.wait_ge(dsum_done, g)
                pe.wait_ge(adj_normed, g + 1)
                nc.tensor.transpose(adj_ps[:, 0:P], adj_in[:, p, :], ident[:, :])
                nc.tensor.transpose(adj_ps[:, P:2 * P], adj_norm[:, :], ident[:, :]).then_inc(adj_transposed, 1)

            def transpose_x(g, p):
                pe.wait_ge(x_loaded[p], loads(g, p))
                if later(g, 1):
                    pe.wait_ge(xT_lo_done, g)
                if later(g, 2):
                    pe.wait_ge(gxT_lo_done, g - 1)
                for k in range(KD):
                    last = nc.tensor.transpose(xt_ps[:, k * P:(k + 1) * P], x_in[:, p, k * P:(k + 1) * P], ident[:, :])
                last.then_inc(x_transposed, 1)

            def aggregate_x(g, p):
                pe.wait_ge(x_loaded[p], loads(g, p))
                if later(g, 1):
                    pe.wait_ge(aggT_lo_done, g)
                if later(g, 2):
                    pe.wait_ge(h_biased[0], g - 1)
                pe.wait_ge(adjT_done, g + 1)
                for k in range(KD):
                    last = nc.tensor.matmul(agg_ps[:, k * P:(k + 1) * P], x_in[:, p, k * P:(k + 1) * P],
                                            adjT_norm[:, :], start=True, stop=True)
                last.then_inc(agg_ready, 1)
                pe.wait_ge(w_col_done, g + 1)
                pe.wait_ge(inc_be_done, g + 1)
                nc.tensor.matmul(adj_ps[:, 0:P + 2], incT[:, :], incT_be[:, :], start=True, stop=True).then_inc(
                    G_ready, 1)

            def layer0(g):
                if later(g, 1):
                    pe.wait_ge(r0_done, g)
                pe.wait_ge(xT_hi_done, g + 1)
                hi_passes(l0_ps, xT_hi, [w0_hi[:, k, :] for k in range(KD)], [w0_lo[:, k, :] for k in range(KD)], True)
                pe.wait_ge(aggT_hi_done, g + 1)
                hi_passes(l0_ps, aggT_hi, [w0_hi[:, k, :] for k in range(KD, K0)],
                          [w0_lo[:, k, :] for k in range(KD, K0)], False)
                pe.wait_ge(xT_lo_done, g + 1)
                lo_passes(l0_ps, xT_lo, [w0_hi[:, k, :] for k in range(KD)], False)
                pe.wait_ge(aggT_lo_done, g + 1)
                lo_passes(l0_ps, aggT_lo, [w0_hi[:, k, :] for k in range(KD, K0)], True).then_inc(l0_ready, 1)

            def aggregate_x1(g, p):
                if later(g, 1):
                    pe.wait_ge(gxT_lo_done, g)
                if within(g + 1, GRAPHS):
                    pe.wait_ge(xT_lo_done, g + 2)
                pe.wait_ge(G_lo_done, g + 1)
                pe.wait_ge(x1_lo_done, g + 1)
                by_G(gx_ps, x1_hi, x1_lo, p).then_inc(gx_ready, 1)

            def layer1_w1(g):
                if within(g + 1, GRAPHS):
                    pe.wait_ge(aggT_lo_done, g + 2)
                for n in range(HALVES):
                    if later(g, 1):
                        pe.wait_ge(h_biased[n], g)
                    elif n == 1:
                        pe.wait_ge(w_lo_done, len(groups))
                    if n == 0:
                        pe.wait_ge(gxT_hi_done, g + 1)
                    cols = slice(n * BANK, (n + 1) * BANK)
                    hi_passes(h_ps[n], gxT_hi, [w1_hi[:, k, cols] for k in range(KD)],
                              [w1_lo[:, k, cols] for k in range(KD)], True)
                    if n == 0:
                        pe.wait_ge(gxT_lo_done, g + 1)
                    lo_passes(h_ps[n], gxT_lo, [w1_hi[:, k, cols] for k in range(KD)], True).then_inc(h_ready[n], 1)

            def aggregate_z(g, p):
                for n in range(2):
                    if later(g, 1):
                        pe.wait_ge(gzT_lo_done[n], g)
                    pe.wait_ge(z_hi_done, g * 2 + (n + 1))
                    pe.wait_ge(z_lo_done, g * 2 + (n + 1))
                    cols = slice(n * BANK, (n + 1) * BANK)
                    by_G(gz_ps[n], z_hi[:, cols], z_lo[:, cols], p).then_inc(gz_ready[n], 1)

            def spread_v():
                pe.wait_ge(v_spread, KD)
                for k in range(KD):
                    last = nc.tensor.matmul(y_ps[:, k * P:(k + 1) * P], ones[:, :], v_diag[:, k, :], start=True,
                                            stop=True)
                last.then_inc(v_ready, 1)

            def layer1_w2(g):
                if later(g, 1):
                    pe.wait_ge(r1_done, g)
                else:
                    pe.wait_ge(v_copied, 1)
                for n in range(2):
                    ks = range(n * KH // 2, (n + 1) * KH // 2)
                    pe.wait_ge(gzT_hi_done[n], g + 1)
                    hi_passes(y_ps, gzT_hi[:, n * BANK:(n + 1) * BANK], [w2_hi[:, k, :] for k in ks],
                              [w2_lo[:, k, :] for k in ks], n == 0)
                pe.wait_ge(gzT_lo_done[0], g + 1)
                lo_passes(y_ps, gzT_lo[:, 0:BANK], [w2_hi[:, k, :] for k in range(KH // 2)], False)

            def layer1_w2_rest(g):
                pe.wait_ge(gzT_lo_done[1], g + 1)
                lo_passes(y_ps, gzT_lo[:, BANK:DH], [w2_hi[:, k, :] for k in range(KH // 2, KH)], True).then_inc(
                    y_ready, 1)

            def transpose_weights(first, end):
                for n in range(first, end):
                    rows, o0, k, _, _ = groups[n]
                    if n in group_loaded:
                        pe.wait_ge(group_loaded[n], 16)
                    if n >= TURNS:
                        pe.wait_ge(w_lo_done, n - TURNS + 1)
                    for o in range(4):
                        last = nc.tensor.transpose(group_ps[n % TURNS][:, o * P:(o + 1) * P],
                                                   rows[:, o0 + o, k * P:(k + 1) * P], ident[:, :])
                    last.then_inc(wT_ready, 1)

            pe.wait_ge(ident_made, 1)
            transpose_adj(0, 0)
            transpose_x(0, 0)
            transpose_weights(0, W1_AT)
            pe.wait_ge(gamma_loaded, 16)
            nc.tensor.transpose(l0_ps[:, 0:KH], gamma_rows[:, :], ident[0:KH, 0:KH]).then_inc(gamma_transposed, 1)
            aggregate_x(0, 0)
            transpose_weights(W1_AT, W1_AT + KD)
            transpose_adj(1, 1)
            transpose_weights(W1_AT + KD, W2_AT + TURNS)
            pe.wait_ge(gamma_copied, 1)
            pe.wait_ge(w_lo_done, W1_AT)
            layer0(0)
            aggregate_x(1, 1)
            transpose_x(1, 1)
            transpose_weights(W2_AT + TURNS, W2_AT + 2 * TURNS)
            aggregate_x1(0, 0)
            transpose_weights(W2_AT + 2 * TURNS, len(groups))
            transpose_adj(2, 0)
            pe.wait_ge(w_lo_done, W2_AT)
            layer1_w1(0)

            def iteration(i, e):
                if not later(i, 1):
                    spread_v()
                if within(i + 1, GRAPHS):
                    layer0(i + 1)
                if within(i + 2, GRAPHS):
                    aggregate_x(i + 2, e)
                aggregate_z(i, e)
                if within(i + 2, GRAPHS):
                    transpose_x(i + 2, e)
                layer1_w2(i)
                if within(i + 1, GRAPHS):
                    aggregate_x1(i + 1, 1 - e)
                layer1_w2_rest(i)
                if within(i + 3, GRAPHS):
                    transpose_adj(i + 3, 1 - e)
                if within(i + 1, GRAPHS):
                    layer1_w1(i + 1)

            iteration(0, 0)
            iteration(1, 1)
            with pe.Fori(2, GRAPHS - 4, 2) as i:
                for e in range(2):
                    iteration(i + e if e else i, e)
            for i in range(GRAPHS - 4, GRAPHS):
                iteration(i, i % 2)

        @block.scalar
        def _(act):
            def relu(g, n):
                act.wait_ge(h_biased[n], g + 1)
                c = slice(n * BANK, (n + 1) * BANK)
                nc.scalar.activation(h[:, c], h[:, c], ACT.Relu).then_inc(h_relued[n], 1)

            def root_h(g):
                act.wait_ge(mvh_done, g + 1)
                if later(g, 1):
                    act.wait_ge(nbh_done, g)
                    act.wait_ge(z_done, g * 2)
                nc.scalar.activation(sdh[:, 0:1], mvh[:, 1:2], ACT.Sqrt, bias=eps_scaled[:, :],
                                     scale=PART_SCALE ** -2).then_inc(sdh_done, 1)

            def z_high(g):
                act.wait_ge(nbh_done, g + 1)
                for n in range(2):
                    if later(g, 1):
                        act.wait_ge(gz_ready[n], g)
                    c = slice(n * BANK, (n + 1) * BANK)
                    nc.scalar.activation(z_hi[:, c], h[:, c], ACT.Identity, bias=nbh[:, :], scale=sdh[:, 1:2]).then_inc(
                        z_hi_done, 1)

            def gzT_high(g):
                for n in range(2):
                    act.wait_ge(gz_ready[n], g + 1)
                    if later(g, 1):
                        act.wait_ge(y_ready, g)
                    c = slice(n * BANK, (n + 1) * BANK)
                    nc.scalar.activation(gzT_hi[:, c], gz_ps[n][:, :], ACT.Identity).then_inc(gzT_hi_done[n], 1)

            def root0(g):
                act.wait_ge(mv0_done, g + 1)
                nc.scalar.activation(sd0[:, 0:1], mv0[:, 1:2], ACT.Sqrt, bias=eps_col[:, :]).then_inc(sd0_done, 1)

            def x1_high(g, p):
                act.wait_ge(x1_done, g + 1)
                if later(g, 1):
                    act.wait_ge(gx_ready, g)
                nc.scalar.activation(x1_hi[:, :], x1[:, p, :], ACT.Identity, scale=PART_SCALE).then_inc(x1_hi_done, 1)

            def G_high(g, p):
                act.wait_ge(G_ready, g + 1)
                if later(g, 2):
                    act.wait_ge(gz_ready[1], g - 1)
                nc.scalar.activation(G_hi[:, p, :], adj_ps[:, 0:P], ACT.Identity, scale=PART_SCALE).then_inc(
                    G_hi_done, 1)

            def xT_high(g):
                act.wait_ge(x_transposed, g + 1)
                if later(g, 1):
                    act.wait_ge(l0_ready, g)
                nc.scalar.activation(xT_hi[:, :], xt_ps[:, :], ACT.Identity).then_inc(xT_hi_done, 1)

            def gxT_high(g):
                act.wait_ge(gx_ready, g + 1)
                if later(g, 1):
                    act.wait_ge(h_ready[1], g)
                nc.scalar.activation(gxT_hi[:, :], gx_ps[:, :], ACT.Identity).then_inc(gxT_hi_done, 1)

            def aggT_high(g):
                act.wait_ge(agg_ready, g + 1)
                if later(g, 1):
                    act.wait_ge(l0_ready, g)
                nc.scalar.activation(aggT_hi[:, :], agg_ps[:, :], ACT.Identity).then_inc(aggT_hi_done, 1)

            def root1(g):
                act.wait_ge(mv1_done, g + 1)
                nc.scalar.activation(sd1[:, 0:1], mv1[:, 1:2], ACT.Sqrt, bias=eps_col[:, :]).then_inc(sd1_done, 1)

            def normalise_out(g, p):
                act.wait_ge(nb1_done, g + 1)
                if later(g, 2):
                    act.wait_ge(stored[p], loads(g, p) - 16)
                nc.scalar.activation(y_out[:, p, :], r1[:, :], ACT.Identity, bias=nb1[:, :], scale=sd1[:, 1:2]).then_inc(
                    y_done, 1)

            def weights_high(first, end):
                for n in range(first, end):
                    _, _, k, hi, _ = groups[n]
                    act.wait_ge(wT_ready, n + 1)
                    if n >= W2_AT:
                        nc.scalar.activation(hi, group_ps[n % TURNS][:, :], ACT.Identity,
                                             scale=gamma_cols[:, k:k + 1]).then_inc(w_hi_done, 1)
                    else:
                        nc.scalar.activation(hi, group_ps[n % TURNS][:, :], ACT.Identity).then_inc(w_hi_done, 1)

            act.wait_ge(consts, 5)
            nc.scalar.activation(root_warm[:, :], eps_col[:, :], ACT.Sqrt)
            xT_high(0)
            weights_high(0, W1_AT)
            G_high(0, 0)
            aggT_high(0)
            act.wait_ge(gamma_copied, 1)
            weights_high(W1_AT, W2_AT + TURNS)
            aggT_high(1)
            root0(0)
            xT_high(1)
            x1_high(0, 0)
            G_high(1, 1)
            weights_high(W2_AT + TURNS, W2_AT + 2 * TURNS)
            gxT_high(0)
            weights_high(W2_AT + 2 * TURNS, len(groups))
            for k in range(KD):
                act.wait_ge(v_product_done, k + 1)
                nc.scalar.activation(stage_b[:, k * DH:(k + 1) * DH], stage_b[:, k * DH:(k + 1) * DH], ACT.Identity,
                                     accum_out=v_cols[:, k:k + 1]).then_inc(v_summed, 1)
            relu(0, 0)

            def iteration(i, e):
                root_h(i)
                z_high(i)
                if within(i + 2, GRAPHS):
                    aggT_high(i + 2)
                gzT_high(i)
                if within(i + 2, GRAPHS):
                    xT_high(i + 2)
                if within(i + 1, GRAPHS):
                    root0(i + 1)
                if within(i + 2, GRAPHS):
                    G_high(i + 2, e)
                if within(i + 1, GRAPHS):
                    x1_high(i + 1, 1 - e)
                    gxT_high(i + 1)
                root1(i)
                normalise_out(i, e)
                if within(i + 1, GRAPHS):
                    relu(i + 1, 0)

            iteration(0, 0)
            iteration(1, 1)
            with act.Fori(2, GRAPHS - 4, 2) as i:
                for e in range(2):
                    iteration(i + e if e else i, e)
            for i in range(GRAPHS - 4, GRAPHS):
                iteration(i, i % 2)

        @block.vector
        def _(dve):
            def sum_adj(g, p):
                dve.wait_ge(adj_loaded[p], loads(g, p))
                nc.vector.reduce_sum(deg[:, 0:1], adj_in[:, p, :], axis=AX_X).then_inc(deg_summed, 1)

            def invert_deg(g, h_stats=None):
                dve.wait_ge(deg_summed, g + 1)
                if h_stats is not None:
                    dve.wait_ge(sth_done, h_stats * 2 + 2)
                nc.vector.tensor_scalar_max(deg[:, 1:2], deg[:, 0:1], DEG_EPS).then_inc(deg_guarded, 1)
                if h_stats is not None:
                    aggregate_h()
                dve.wait_ge(deg_guarded, g + 1)
                nc.vector.reciprocal(deg[:, 2:3], deg[:, 1:2]).then_inc(deg_inverted, 1)

            def scale_adj(g, p):
                if later(g, 1):
                    dve.wait_ge(adj_transposed, g)
                dve.wait_ge(deg_inverted, g + 1)
                nc.vector.tensor_scalar_mul(adj_norm[:, :], adj_in[:, p, :], deg[:, 2:3]).then_inc(adj_normed, 1)

            def incidence(g, stats1=None):
                dve.wait_ge(adj_transposed, g + 1)
                if later(g, 1):
                    dve.wait_ge(agg_ready, g)
                    dve.wait_ge(G_ready, g)
                if stats1 is not None:
                    dve.wait_ge(st1_done, stats1 + 1)
                nc.vector.tensor_scalar(incT[:, :], adj_ps[:, 0:P], 0.0, 0.0, ALU.not_equal, ALU.add,
                                        accum_out=count[:, 0:1]).then_inc(inc_made, 1)
                if stats1 is not None:
                    aggregate1()
                nc.vector.tensor_copy(adjT_norm[:, :], adj_ps[:, P:2 * P]).then_inc(adjT_done, 1)
                nc.vector.tensor_copy(incT_be[:, P:P + 1], adj_ps[:, 0:1]).then_inc(w_col_done, 1)
                dve.wait_ge(inc_made, g + 1)
                nc.vector.tensor_scalar_max(count[:, 1:2], count[:, 0:1], 1.0).then_inc(count_guarded, 1)
                dve.wait_ge(count_guarded, g + 1)
                nc.vector.reciprocal(count[:, 2:3], count[:, 1:2]).then_inc(count_inverted, 1)
                dve.wait_ge(count_inverted, g + 1)
                nc.vector.tensor_scalar_mul(incT_be[:, 0:P], incT[:, :], count[:, 2:3]).then_inc(inc_be_done, 1)

            def copy_G(g, p):
                dve.wait_ge(G_hi_done, g + 1)
                if later(g, 2):
                    dve.wait_ge(gz_ready[1], g - 1)
                nc.vector.scalar_tensor_tensor(out=G_lo[:, p, :], in0=adj_ps[:, 0:P], scalar=PART_SCALE,
                                               in1=G_hi[:, p, :], op0=ALU.mult, op1=ALU.subtract).then_inc(
                    G_lo_done, 1)
                if later(g, 1):
                    dve.wait_ge(dq_done, g)
                nc.vector.tensor_copy(dsum[:, :], adj_ps[:, P:P + 2]).then_inc(dsum_done, 1)

            def degrees(g, p):
                dve.wait_ge(dsum_done, g + 1)
                nc.vector.tensor_scalar_max(dcol[:, 0:1], dsum[:, 0:1], TINY).then_inc(d_guarded, 1)
                nc.vector.tensor_scalar(dcol[:, 1:2], dsum[:, 0:1], 0.0, PART_SCALE ** -2, ALU.is_gt,
                                        ALU.mult).then_inc(d_positive, 1)
                dve.wait_ge(d_guarded, g + 1)
                nc.vector.reciprocal(dcol[:, 2:3], dcol[:, 0:1]).then_inc(d_inverted, 1)
                dve.wait_ge(d_positive, g + 1)
                dve.wait_ge(d_inverted, g + 1)
                nc.vector.tensor_tensor(dn[:, p, 0:1], dcol[:, 1:2], dcol[:, 2:3], ALU.mult).then_inc(dn_done, 1)
                dve.wait_ge(dn_done, g + 1)
                nc.vector.scalar_tensor_tensor(out=dn[:, p, 1:2], in0=dn[:, p, 0:1], scalar=PART_SCALE ** 2,
                                               in1=dsum[:, 1:2], op0=ALU.mult, op1=ALU.mult).then_inc(dq_done, 1)

            def xT_low(g):
                dve.wait_ge(xT_hi_done, g + 1)
                nc.vector.tensor_tensor(xT_lo[:, :], xt_ps[:, :], xT_hi[:, :].bitcast(F32), ALU.subtract).then_inc(
                    xT_lo_done, 1)

            def aggT_low(g, stats0=None):
                dve.wait_ge(aggT_hi_done, g + 1)
                if stats0 is not None:
                    dve.wait_ge(st0_done, stats0 + 1)
                nc.vector.tensor_tensor(aggT_lo[:, :], agg_ps[:, :], aggT_hi[:, :].bitcast(F32),
                                        ALU.subtract).then_inc(aggT_lo_done, 1)
                if stats0 is not None:
                    aggregate0()

            def gxT_low(g):
                dve.wait_ge(gxT_hi_done, g + 1)
                nc.vector.tensor_tensor(gxT_lo[:, :], gx_ps[:, :], gxT_hi[:, :].bitcast(F32),
                                        ALU.subtract).then_inc(gxT_lo_done, 1)

            def gzT_low(g):
                for n in range(2):
                    dve.wait_ge(gzT_hi_done[n], g + 1)
                    c = slice(n * BANK, (n + 1) * BANK)
                    nc.vector.tensor_tensor(gzT_lo[:, c], gz_ps[n][:, :], gzT_hi[:, c].bitcast(F32),
                                            ALU.subtract).then_inc(gzT_lo_done[n], 1)

            def residual0(g, p):
                dve.wait_ge(l0_ready, g + 1)
                if later(g, 1):
                    dve.wait_ge(x1_done, g)
                nc.vector.scalar_tensor_tensor(out=r0[:, :], in0=l0_ps[:, :], scalar=0.0, in1=x_in[:, p, :],
                                               op0=ALU.max, op1=ALU.add).then_inc(r0_done, 1)
                dve.wait_ge(r0_done, g + 1)
                nc.vector.bn_stats(st0[:, :], r0[:, :]).then_inc(st0_done, 1)

            def aggregate0():
                nc.vector.bn_aggr(mv0[:, :], st0[:, :]).then_inc(mv0_done, 1)

            def normalise_x1(g, p):
                dve.wait_ge(sd0_done, g + 1)
                nc.vector.reciprocal(sd0[:, 1:2], sd0[:, 0:1]).then_inc(rs0_done, 1)
                dve.wait_ge(rs0_done, g + 1)
                if later(g, 2):
                    dve.wait_ge(base_done, g - 1)
                nc.vector.tensor_scalar(x1[:, p, :], r0[:, :], mv0[:, 0:1], sd0[:, 1:2], ALU.subtract,
                                        ALU.mult).then_inc(x1_done, 1)

            def x1_low(g, p):
                dve.wait_ge(x1_hi_done, g + 1)
                nc.vector.scalar_tensor_tensor(out=x1_lo[:, :], in0=x1[:, p, :], scalar=PART_SCALE, in1=x1_hi[:, :],
                                               op0=ALU.mult, op1=ALU.subtract).then_inc(x1_lo_done, 1)

            def z_low(g):
                for n in range(2):
                    c = slice(n * BANK, (n + 1) * BANK)
                    if later(g, 1):
                        dve.wait_ge(z_lo_done, g * 2)
                    dve.wait_ge(rsh_done, g + 1)
                    nc.vector.tensor_scalar(z[:, c], h[:, c], mvh[:, 0:1], sdh[:, 1:2], ALU.subtract,
                                            ALU.mult).then_inc(z_done, 1)
                for n in range(2):
                    c = slice(n * BANK, (n + 1) * BANK)
                    dve.wait_ge(z_done, g * 2 + 2)
                    dve.wait_ge(z_hi_done, g * 2 + (n + 1))
                    nc.vector.tensor_tensor(z_lo[:, c], z[:, c], z_hi[:, c], ALU.subtract).then_inc(z_lo_done, 1)

            def bias_h(g, p, n):
                dve.wait_ge(h_ready[n], g + 1)
                dve.wait_ge(dn_done, g + 1)
                if later(g, 1):
                    dve.wait_ge(z_hi_done, g * 2)
                    dve.wait_ge(z_done, g * 2)
                c = slice(n * BANK, (n + 1) * BANK)
                nc.vector.scalar_tensor_tensor(out=h[:, c], in0=h_ps[n][:, :], scalar=dn[:, p, 0:1], in1=b1_all[:, c],
                                               op0=ALU.mult, op1=ALU.add).then_inc(h_biased[n], 1)

            def relu1(g):
                dve.wait_ge(h_biased[1], g + 1)
                nc.vector.tensor_scalar_max(h[:, BANK:DH], h[:, BANK:DH], 0.0).then_inc(h_relued[1], 1)

            def stats_h(g, n):
                dve.wait_ge(h_relued[n], g + 1)
                nc.vector.bn_stats(sth[:, n, :], h[:, n * BANK:(n + 1) * BANK]).then_inc(sth_done, 1)

            def aggregate_h():
                nc.vector.bn_aggr(mvh[:, :], sth[:, :, :].rearrange("p a b -> p (a b)")).then_inc(mvh_done, 1)

            def scales_h(g):
                dve.wait_ge(sdh_done, g + 1)
                nc.vector.reciprocal(sdh[:, 1:2], sdh[:, 0:1]).then_inc(rsh_done, 1)
                dve.wait_ge(rsh_done, g + 1)
                nc.vector.scalar_tensor_tensor(out=nbh[:, :], in0=mvh[:, 0:1], scalar=-1.0, in1=sdh[:, 1:2],
                                               op0=ALU.mult, op1=ALU.mult).then_inc(nbh_done, 1)

            def base(g, p):
                dve.wait_ge(dq_done, g + 1)
                if later(g, 1):
                    dve.wait_ge(base_done, g)
                nc.vector.scalar_tensor_tensor(out=bias_y[:, :], in0=v_all[:, :], scalar=dn[:, p, 1:2], in1=b2_all[:, :],
                                               op0=ALU.mult, op1=ALU.add).then_inc(bias_done, 1)
                dve.wait_ge(bias_done, g + 1)
                dve.wait_ge(x1_done, g + 1)
                if later(g, 1):
                    dve.wait_ge(r1_done, g)
                nc.vector.scalar_tensor_tensor(out=base_y[:, :], in0=x1[:, p, :], scalar=2.0, in1=bias_y[:, :],
                                               op0=ALU.mult, op1=ALU.add).then_inc(base_done, 1)

            def residual1(g, p):
                dve.wait_ge(y_ready, g + 1)
                dve.wait_ge(base_done, g + 1)
                if later(g, 1):
                    dve.wait_ge(y_done, g)
                nc.vector.scalar_tensor_tensor(out=r1[:, :], in0=y_ps[:, :], scalar=dn[:, p, 0:1], in1=base_y[:, :],
                                               op0=ALU.mult, op1=ALU.add).then_inc(r1_done, 1)
                dve.wait_ge(r1_done, g + 1)
                nc.vector.bn_stats(st1[:, :], r1[:, :]).then_inc(st1_done, 1)

            def aggregate1():
                nc.vector.bn_aggr(mv1[:, :], st1[:, :]).then_inc(mv1_done, 1)

            def scales1(g):
                dve.wait_ge(sd1_done, g + 1)
                nc.vector.reciprocal(sd1[:, 1:2], sd1[:, 0:1]).then_inc(rs1_done, 1)
                dve.wait_ge(rs1_done, g + 1)
                nc.vector.scalar_tensor_tensor(out=nb1[:, :], in0=mv1[:, 0:1], scalar=-1.0, in1=sd1[:, 1:2],
                                               op0=ALU.mult, op1=ALU.mult).then_inc(nb1_done, 1)

            def weights_low(first, end):
                for n in range(first, end):
                    _, _, k, hi, lo = groups[n]
                    dve.wait_ge(w_hi_done, n + 1)
                    if n >= W2_AT:
                        nc.vector.scalar_tensor_tensor(out=lo, in0=group_ps[n % TURNS][:, :],
                                                       scalar=gamma_cols[:, k:k + 1], in1=hi.bitcast(F32),
                                                       op0=ALU.mult, op1=ALU.subtract).then_inc(w_lo_done, 1)
                    else:
                        nc.vector.tensor_tensor(lo, group_ps[n % TURNS][:, :], hi.bitcast(F32),
                                                ALU.subtract).then_inc(w_lo_done, 1)

            sum_adj(0, 0)
            invert_deg(0)
            scale_adj(0, 0)
            dve.wait_ge(consts, 5)
            incidence(0)
            xT_low(0)
            weights_low(0, W1_AT)
            sum_adj(1, 1)
            invert_deg(1)
            scale_adj(1, 1)
            copy_G(0, 0)
            dve.wait_ge(gamma_transposed, 1)
            nc.vector.tensor_copy(gamma_cols[:, :], l0_ps[:, 0:KH]).then_inc(gamma_copied, 1)
            aggT_low(0)
            weights_low(W1_AT, W1_AT + KD)
            incidence(1)
            weights_low(W1_AT + KD, W2_AT + TURNS)
            degrees(0, 0)
            sum_adj(2, 0)
            invert_deg(2)
            scale_adj(2, 0)
            residual0(0, 0)
            aggT_low(1, stats0=0)
            normalise_x1(0, 0)
            xT_low(1)
            x1_low(0, 0)
            copy_G(1, 1)
            weights_low(W2_AT + TURNS, W2_AT + 2 * TURNS)
            gxT_low(0)
            weights_low(W2_AT + 2 * TURNS, len(groups))
            incidence(2)
            degrees(1, 1)
            dve.wait_ge(v_summed, KD)
            dve.wait_ge(ident_made, 1)
            for k in range(KD):
                nc.vector.tensor_scalar_mul(v_diag[:, k, :], ident[:, :], v_cols[:, k:k + 1]).then_inc(v_spread, 1)
            dve.wait_ge(bias_loaded, 32)
            bias_h(0, 0, 0)
            sum_adj(3, 1)
            stats_h(0, 0)

            def iteration(i, e):
                bias_h(i, e, 1)
                relu1(i)
                stats_h(i, 1)
                if within(i + 3, GRAPHS):
                    invert_deg(i + 3, h_stats=i)
                else:
                    dve.wait_ge(sth_done, i * 2 + 2)
                    aggregate_h()
                scales_h(i)
                z_low(i)
                if not later(i, 1):
                    dve.wait_ge(v_ready, 1)
                    nc.vector.tensor_copy(v_all[:, :], y_ps[:, :]).then_inc(v_copied, 1)
                if within(i + 1, GRAPHS):
                    residual0(i + 1, 1 - e)
                if within(i + 2, GRAPHS):
                    aggT_low(i + 2, stats0=i + 1)
                elif within(i + 1, GRAPHS):
                    dve.wait_ge(st0_done, i + 2)
                    aggregate0()
                gzT_low(i)
                if within(i + 1, GRAPHS):
                    normalise_x1(i + 1, 1 - e)
                if within(i + 2, GRAPHS):
                    xT_low(i + 2)
                    copy_G(i + 2, e)
                if within(i + 1, GRAPHS):
                    x1_low(i + 1, 1 - e)
                if not later(i, 1):
                    dve.wait_ge(v_copied, 1)
                base(i, e)
                if within(i + 3, GRAPHS):
                    scale_adj(i + 3, 1 - e)
                if within(i + 1, GRAPHS):
                    gxT_low(i + 1)
                residual1(i, e)
                if within(i + 3, GRAPHS):
                    incidence(i + 3, stats1=i)
                else:
                    dve.wait_ge(st1_done, i + 1)
                    aggregate1()
                scales1(i)
                if within(i + 2, GRAPHS):
                    degrees(i + 2, e)
                if within(i + 1, GRAPHS):
                    bias_h(i + 1, 1 - e, 0)
                    if within(i + 4, GRAPHS):
                        sum_adj(i + 4, e)
                    stats_h(i + 1, 0)

            iteration(0, 0)
            iteration(1, 1)
            with dve.Fori(2, GRAPHS - 4, 2) as i:
                for e in range(2):
                    iteration(i + e if e else i, e)
            for i in range(GRAPHS - 4, GRAPHS):
                iteration(i, i % 2)


_INS = ["x", "adj", "L0_gnn_W", "L1_gnn_W1", "L1_gnn_b1", "L1_gnn_gamma", "L1_gnn_beta", "L1_gnn_W2", "L1_gnn_b2"]


def kernel(**inputs):
    import numpy as np
    import concourse.bacc as bacc
    from concourse.bass_utils import run_bass_kernel_spmd

    nc = bacc.Bacc("TRN2", target_bir_lowering=False, num_devices=1)
    arrays, args = {}, []
    for name in _INS:
        a = np.ascontiguousarray(inputs[name])
        arrays[f"in_{name}"] = a
        args.append(nc.dram_tensor(f"in_{name}", a.shape, mybir.dt.from_np(a.dtype), kind="ExternalInput").ap())
    out = nc.dram_tensor("out_0", inputs["x"].shape, F32, kind="ExternalOutput").ap()
    two_layer_graph_kernel(nc, *args, out)
    r = run_bass_kernel_spmd(nc, [arrays], core_ids=[0])
    return r.results[0]["out_0"]
```

```python
from contextlib import ExitStack

import concourse.bass as bass
from concourse import mybir

P = 128
BANK = 512

ALU = mybir.AluOpType
ACT = mybir.ActivationFunctionType
F32 = mybir.dt.float32
F32R = mybir.dt.float32r
F16 = mybir.dt.float16
AX_X = mybir.AxisListType.X

DEG_EPS = 1e-6
LN_EPS = 1e-5
PART_SCALE = 256.0
TINY = 1.1754944e-38


def later(g, n):
    return not isinstance(g, int) or g >= n


def within(g, graphs):
    return not isinstance(g, int) or g < graphs


def loads(g, p):
    return (g - p) * 8 + 16


def two_layer_graph_kernel(nc, x_pair, adj_pair, W0T, W1T, b1, gamma_beta, W2T, b2, out):
    GRAPHS, NODES, D = out.shape
    DH = W1T.shape[1]
    KD = D // P
    KH = DH // P
    K0 = 2 * KD
    HALVES = DH // BANK
    ADJ_AHEAD, X_AHEAD = 4, 3
    assert NODES == P and D == BANK and DH == 2 * BANK and GRAPHS % 2 == 0 and GRAPHS >= 8

    with ExitStack() as ctx:
        def sb(name, shape, dt=F32):
            return ctx.enter_context(nc.sbuf_tensor(name, shape, dt))

        def sem(name):
            return ctx.enter_context(nc.semaphore(name))

        w0_hi = sb("w0_hi", [P, K0, D], F32R)
        w0_lo = sb("w0_lo", [P, K0, D], F32R)
        w1_hi = sb("w1_hi", [P, KD, DH], F32R)
        w1_lo = sb("w1_lo", [P, KD, DH], F32R)
        w2_hi = sb("w2_hi", [P, KH, D], F32R)
        w2_lo = sb("w2_lo", [P, KH, D], F32R)
        stage_a = sb("stage_a", [P, K0, D])
        stage_b = sb("stage_b", [P, KD, DH])
        scales = sb("scales", [P, 2, KH])
        v_sum = sb("v_sum", [P, D])
        ident = sb("ident", [P, P])
        ones = sb("ones", [P, P])
        eps_col = sb("eps_col", [P, 1])
        root_warm = sb("root_warm", [P, 1])
        eps_scaled = sb("eps_scaled", [P, 1])
        b1_all = sb("b1_all", [P, DH])
        b2_all = sb("b2_all", [P, D])
        v_all = sb("v_all", [P, D])

        x_in = sb("x_in", [P, 2, 2 * D])
        adj_in = sb("adj_in", [P, 2, 2 * P])
        adj_norm = sb("adj_norm", [P, P])
        deg = sb("deg", [P, 3])
        adjT_hi = sb("adjT_hi", [P, P], F32R)
        adjT_lo = sb("adjT_lo", [P, P], F32R)
        incT = sb("incT", [P, P])
        count = sb("count", [P, 3])
        incT_be = sb("incT_be", [P, P + 2])
        G_hi = sb("G_hi", [P, 2, P], F16)
        G_lo = sb("G_lo", [P, 2, P], F16)
        dsum = sb("dsum", [P, 2])
        dcol = sb("dcol", [P, 3])
        dn = sb("dn", [P, 2, 2])
        xT_hi = sb("xT_hi", [P, D], F32R)
        xT_lo = sb("xT_lo", [P, D], F32R)
        xw_hi = sb("xw_hi", [P, D], F32R)
        xw_lo = sb("xw_lo", [P, D], F32R)
        r0 = sb("r0", [P, D])
        x1 = sb("x1", [P, 2, D])
        x1_hi = sb("x1_hi", [P, D], F16)
        x1_lo = sb("x1_lo", [P, D], F16)
        gxT_hi = sb("gxT_hi", [P, D], F32R)
        gxT_lo = sb("gxT_lo", [P, D], F32R)
        h = sb("h", [P, DH])
        z = sb("z", [P, DH])
        z_hi = sb("z_hi", [P, DH], F16)
        z_lo = sb("z_lo", [P, DH], F16)
        gzT_hi = sb("gzT_hi", [P, DH], F32R)
        gzT_lo = sb("gzT_lo", [P, DH], F32R)
        bias_y = sb("bias_y", [P, D])
        base_y = sb("base_y", [P, D])
        r1 = sb("r1", [P, D])
        y_out = sb("y_out", [P, 2, D])
        st0 = sb("st0", [P, 6])
        st1 = sb("st1", [P, 6])
        sth = sb("sth", [P, HALVES, 6])
        mv0 = sb("mv0", [P, 2])
        mv1 = sb("mv1", [P, 2])
        mvh = sb("mvh", [P, 2])
        sd0 = sb("sd0", [P, 2])
        sd1 = sb("sd1", [P, 2])
        sdh = sb("sdh", [P, 2])
        nb1 = sb("nb1", [P, 1])
        nbh = sb("nbh", [P, 1])

        def bank(name):
            return ctx.enter_context(nc.psum_tensor(name, [P, BANK], F32))

        l0_ps = bank("l0_ps")
        h_ps = [bank("h_ps0"), bank("h_ps1")]
        y_ps = bank("y_ps")
        adj_ps = bank("adj_ps")
        gx_ps = bank("gx_ps")
        gz_ps = [bank("gz_ps0"), bank("gz_ps1")]
        xw_ps = h_ps[0]

        PIECES = 4
        w0_loaded = [sem(f"w0_loaded{j}") for j in range(PIECES)]
        w1_loaded = [sem(f"w1_loaded{j}") for j in range(PIECES)]
        w2_loaded = [sem(f"w2_loaded{j}") for j in range(PIECES)]
        scales_loaded, bias_loaded = sem("scales_loaded"), sem("bias_loaded")
        consts, ident_made = sem("consts"), sem("ident_made")
        w_hi_done, w_lo_done = sem("w_hi_done"), sem("w_lo_done")
        v_multiplied, v_added = sem("v_multiplied"), sem("v_added")
        v_ready, v_copied = sem("v_ready"), sem("v_copied")
        x_loaded = [sem("x_loaded0"), sem("x_loaded1")]
        adj_loaded = [sem("adj_loaded0"), sem("adj_loaded1")]
        stored = [sem("stored0"), sem("stored1")]
        deg_summed, deg_guarded, deg_inverted = sem("deg_summed"), sem("deg_guarded"), sem("deg_inverted")
        adj_normed = sem("adj_normed")
        adj_transposed = sem("adj_transposed")
        inc_made, count_guarded, count_inverted = sem("inc_made"), sem("count_guarded"), sem("count_inverted")
        adjT_hi_done, adjT_lo_done = sem("adjT_hi_done"), sem("adjT_lo_done")
        inc_be_done, w_col_done = sem("inc_be_done"), sem("w_col_done")
        xT_hi_done, xT_lo_done = sem("xT_hi_done"), sem("xT_lo_done")
        xw_ready, xw_hi_done, xw_lo_done = sem("xw_ready"), sem("xw_hi_done"), sem("xw_lo_done")
        G_ready, G_hi_done, G_lo_done, dsum_done = (
            sem("G_ready"), sem("G_hi_done"), sem("G_lo_done"), sem("dsum_done"))
        d_guarded, d_positive, d_inverted, dn_done, dq_done = (
            sem("d_guarded"), sem("d_positive"), sem("d_inverted"), sem("dn_done"), sem("dq_done"))
        l0_ready, r0_done, st0_done, mv0_done, sd0_done, rs0_done, x1_done = (
            sem("l0_ready"), sem("r0_done"), sem("st0_done"), sem("mv0_done"), sem("sd0_done"),
            sem("rs0_done"), sem("x1_done"))
        x1_hi_done, x1_lo_done = sem("x1_hi_done"), sem("x1_lo_done")
        gx_ready, gxT_hi_done, gxT_lo_done = sem("gx_ready"), sem("gxT_hi_done"), sem("gxT_lo_done")
        h_ready = [sem("h_ready0"), sem("h_ready1")]
        h_biased = [sem("h_biased0"), sem("h_biased1")]
        h_relued = [sem("h_relued0"), sem("h_relued1")]
        sth_done, mvh_done, sdh_done, rsh_done, nbh_done = (
            sem("sth_done"), sem("mvh_done"), sem("sdh_done"), sem("rsh_done"), sem("nbh_done"))
        z_done, z_hi_done, z_lo_done = sem("z_done"), sem("z_hi_done"), sem("z_lo_done")
        gz_ready = [sem("gz_ready0"), sem("gz_ready1")]
        gzT_hi_done = [sem("gzT_hi_done0"), sem("gzT_hi_done1")]
        gzT_lo_done = [sem("gzT_lo_done0"), sem("gzT_lo_done1")]
        bias_done, base_done = sem("bias_done"), sem("base_done")
        y_ready, r1_done, st1_done, mv1_done, sd1_done, rs1_done, nb1_done, y_done = (
            sem("y_ready"), sem("r1_done"), sem("st1_done"), sem("mv1_done"), sem("sd1_done"),
            sem("rs1_done"), sem("nb1_done"), sem("y_done"))

        W0_ORDER = [2, 3, 0, 1]
        parts = []
        for j in W0_ORDER:
            ks = slice(j * K0 // PIECES, (j + 1) * K0 // PIECES)
            parts.append((stage_a[:, ks, :], w0_hi[:, ks, :], w0_lo[:, ks, :], None, w0_loaded[j]))
        for j in range(PIECES):
            ks = slice(j * KD // PIECES, (j + 1) * KD // PIECES)
            parts.append((stage_b[:, ks, :], w1_hi[:, ks, :], w1_lo[:, ks, :], None, w1_loaded[j]))
        for k in range(KH):
            parts.append((stage_a[:, k, :], w2_hi[:, k, :], w2_lo[:, k, :], k, w2_loaded[k * PIECES // KH]))
        v_terms = stage_b[:, :, :].rearrange("p k (h n) -> p (k h) n", n=D)
        W1_AT, W2_AT = PIECES, 2 * PIECES

        block = ctx.enter_context(nc.Block())

        @block.sync
        def _(sp):
            def load_adj(g, p):
                if later(g, 2):
                    sp.wait_ge(adj_normed, g - 1)
                    sp.wait_ge(inc_made, g - 1)
                    sp.wait_ge(w_col_done, g - 1)
                sp.dma_start(adj_in[:, p, :], adj_pair[g]).then_inc(adj_loaded[p], 16)

            def load_x(g, p):
                if later(g, 2):
                    sp.wait_ge(r0_done, g - 1)
                    sp.wait_ge(xT_lo_done, g - 1)
                sp.dma_start(x_in[:, p, :], x_pair[g]).then_inc(x_loaded[p], 16)

            def store(g, p):
                sp.wait_ge(y_done, g + 1)
                sp.dma_start(out[g], y_out[:, p, :]).then_inc(stored[p], 16)

            def iteration(i, e):
                if within(i + ADJ_AHEAD, GRAPHS):
                    load_adj(i + ADJ_AHEAD, e)
                if within(i + X_AHEAD, GRAPHS):
                    load_x(i + X_AHEAD, 1 - e)
                store(i, e)

            load_adj(0, 0)
            load_x(0, 0)
            w0_dram = W0T.rearrange("(k p) n -> p k n", p=P)
            w1_dram = W1T.rearrange("(k p) n -> p k n", p=P)
            w2_dram = W2T.rearrange("(k p) n -> p k n", p=P)
            for j in W0_ORDER:
                ks = slice(j * K0 // PIECES, (j + 1) * K0 // PIECES)
                sp.dma_start(stage_a[:, ks, :], w0_dram[:, ks, :]).then_inc(w0_loaded[j], 16)
            load_adj(1, 1)
            for j in range(PIECES):
                ks = slice(j * KD // PIECES, (j + 1) * KD // PIECES)
                sp.dma_start(stage_b[:, ks, :], w1_dram[:, ks, :]).then_inc(w1_loaded[j], 16)
            load_x(1, 1)
            for j in range(PIECES):
                sp.wait_ge(w_lo_done, W0_ORDER.index(j) + 1)
                ks = slice(j * KH // PIECES, (j + 1) * KH // PIECES)
                sp.dma_start(stage_a[:, ks, :], w2_dram[:, ks, :]).then_inc(w2_loaded[j], 16)
            load_adj(2, 0)
            load_adj(3, 1)
            load_x(2, 0)
            iteration(0, 0)
            iteration(1, 1)
            with sp.Fori(2, GRAPHS - ADJ_AHEAD - 2, 2) as i:
                for e in range(2):
                    iteration(i + e if e else i, e)
            for i in range(GRAPHS - ADJ_AHEAD - 2, GRAPHS):
                iteration(i, i % 2)
            sp.wait_ge(stored[0], 8 * GRAPHS)
            sp.wait_ge(stored[1], 8 * GRAPHS)

        @block.gpsimd
        def _(pool):
            nc.gpsimd.memset(ident[:, :], 0.0).then_inc(consts, 1)
            nc.gpsimd.memset(ones[:, :], 1.0).then_inc(consts, 1)
            nc.gpsimd.memset(eps_col[:, :], LN_EPS).then_inc(consts, 1)
            nc.gpsimd.memset(eps_scaled[:, :], LN_EPS / PART_SCALE ** 2).then_inc(consts, 1)
            nc.gpsimd.memset(incT_be[:, P + 1:P + 2], 1.0).then_inc(consts, 1)
            pool.wait_ge(consts, 5)
            nc.gpsimd.affine_select(out=ident[:, :], in_=ident[:, :], compare_op=ALU.not_equal, fill=1.0,
                                    base=0, pattern=[[-1, P]], channel_multiplier=1).then_inc(ident_made, 1)
            pool.dma_start(scales[:, :, :], gamma_beta.rearrange("p (a k) -> p a k", a=2)).then_inc(scales_loaded, 16)
            pool.wait_ge(w2_loaded[0], 16)
            pool.dma_start(b1_all[:, :], b1.rearrange("(a n) -> a n", a=1).to_broadcast([P, DH])).then_inc(
                bias_loaded, 16)
            pool.dma_start(b2_all[:, :], b2.rearrange("(a n) -> a n", a=1).to_broadcast([P, D])).then_inc(
                bias_loaded, 16)
            for k in range(1, KH):
                pool.wait_ge(v_multiplied, k + 1)
                if k > 1:
                    pool.wait_ge(v_added, k - 1)
                before = v_terms[:, 0, :] if k == 1 else v_sum[:, :]
                nc.gpsimd.tensor_tensor(v_sum[:, :], before, v_terms[:, k, :], ALU.add).then_inc(v_added, 1)

        @block.tensor
        def _(pe):
            def hi_passes(ps, hi, w_hi, w_lo, first):
                for k in range(len(w_hi)):
                    nc.tensor.matmul(ps[:, :], hi[:, k * P:(k + 1) * P], w_hi[k], start=(first and k == 0), stop=False)
                    nc.tensor.matmul(ps[:, :], hi[:, k * P:(k + 1) * P], w_lo[k], start=False, stop=False)

            def lo_passes(ps, lo, w_hi, last):
                for k in range(len(w_hi)):
                    done = nc.tensor.matmul(ps[:, :], lo[:, k * P:(k + 1) * P], w_hi[k], start=False,
                                            stop=(last and k == len(w_hi) - 1))
                return done

            def hi_by_G(ps, hi, p):
                for k in range(BANK // P):
                    c = slice(k * P, (k + 1) * P)
                    nc.tensor.matmul(ps[:, c], hi[:, c], G_hi[:, p, :], start=(k == 0), stop=False)
                    nc.tensor.matmul(ps[:, c], hi[:, c], G_lo[:, p, :], start=False, stop=False)

            def lo_by_G(ps, lo, p):
                for k in range(BANK // P):
                    c = slice(k * P, (k + 1) * P)
                    done = nc.tensor.matmul(ps[:, c], lo[:, c], G_hi[:, p, :], start=False, stop=(k == BANK // P - 1))
                return done

            def transpose_adj(g):
                pe.wait_ge(G_lo_done, g + 1)
                pe.wait_ge(dsum_done, g + 1)
                pe.wait_ge(adj_normed, g + 1)
                nc.tensor.transpose(adj_ps[:, 0:P], adj_norm[:, :], ident[:, :]).then_inc(adj_transposed, 1)

            def make_G(g):
                if later(g, 1):
                    pe.wait_ge(adjT_lo_done, g)
                pe.wait_ge(w_col_done, g + 1)
                pe.wait_ge(inc_be_done, g + 1)
                nc.tensor.matmul(adj_ps[:, 0:P + 2], incT[:, :], incT_be[:, :], start=True, stop=True).then_inc(
                    G_ready, 1)

            def w0_passes(g, ps, chunks, parts_made):
                half = len(chunks) // 2
                for n in range(2):
                    ks = chunks[n * half:(n + 1) * half]
                    if not later(g, 1):
                        pe.wait_ge(w_lo_done, parts_made - 1 + n)
                    hi_passes(ps, xT_hi[:, n * half * P:], [w0_hi[:, k, :] for k in ks],
                              [w0_lo[:, k, :] for k in ks], n == 0)

            def layer0(g):
                a, b = range(KD), range(KD, K0)
                if later(g, 1):
                    pe.wait_ge(h_biased[0], g)
                pe.wait_ge(xT_hi_done, g + 1)
                w0_passes(g, xw_ps, b, W1_AT // 2)
                pe.wait_ge(xT_lo_done, g + 1)
                lo_passes(xw_ps, xT_lo, [w0_hi[:, k, :] for k in b], True).then_inc(xw_ready, 1)
                if later(g, 1):
                    pe.wait_ge(r0_done, g)
                w0_passes(g, l0_ps, a, W1_AT)
                lo_passes(l0_ps, xT_lo, [w0_hi[:, k, :] for k in a], False)
                pe.wait_ge(adjT_lo_done, g + 1)
                pe.wait_ge(xw_hi_done, g + 1)
                nc.tensor.matmul(l0_ps[:, :], adjT_hi[:, :], xw_hi[:, :], start=False, stop=False)
                nc.tensor.matmul(l0_ps[:, :], adjT_lo[:, :], xw_hi[:, :], start=False, stop=False)
                pe.wait_ge(xw_lo_done, g + 1)
                nc.tensor.matmul(l0_ps[:, :], adjT_hi[:, :], xw_lo[:, :], start=False, stop=True).then_inc(l0_ready, 1)

            def aggregate_x1(g, p):
                if later(g, 1):
                    pe.wait_ge(gxT_lo_done, g)
                if isinstance(g, int) and g == 1:
                    pe.wait_ge(v_copied, 1)
                pe.wait_ge(G_lo_done, g + 1)
                pe.wait_ge(x1_hi_done, g + 1)
                hi_by_G(gx_ps, x1_hi, p)
                pe.wait_ge(x1_lo_done, g + 1)
                lo_by_G(gx_ps, x1_lo, p).then_inc(gx_ready, 1)

            def layer1_w1(g):
                pe.wait_ge(xw_lo_done, g + 1)
                for n in range(HALVES):
                    if later(g, 1):
                        pe.wait_ge(h_biased[n], g)
                    else:
                        pe.wait_ge(w_lo_done, W2_AT)
                    if n == 0:
                        pe.wait_ge(gxT_hi_done, g + 1)
                    cols = slice(n * BANK, (n + 1) * BANK)
                    hi_passes(h_ps[n], gxT_hi, [w1_hi[:, k, cols] for k in range(KD)],
                              [w1_lo[:, k, cols] for k in range(KD)], True)
                    if n == 0:
                        pe.wait_ge(gxT_lo_done, g + 1)
                    lo_passes(h_ps[n], gxT_lo, [w1_hi[:, k, cols] for k in range(KD)], True).then_inc(h_ready[n], 1)

            def aggregate_z(g, p):
                for n in range(2):
                    if later(g, 1):
                        pe.wait_ge(gzT_lo_done[n], g)
                    cols = slice(n * BANK, (n + 1) * BANK)
                    pe.wait_ge(z_hi_done, g * 2 + (n + 1))
                    hi_by_G(gz_ps[n], z_hi[:, cols], p)
                    pe.wait_ge(z_lo_done, g * 2 + (n + 1))
                    lo_by_G(gz_ps[n], z_lo[:, cols], p).then_inc(gz_ready[n], 1)

            def spread_v():
                pe.wait_ge(gxT_lo_done, 1)
                pe.wait_ge(v_added, KH - 1)
                nc.tensor.matmul(gx_ps[:, :], ones[:, :], v_sum[:, :], start=True, stop=True).then_inc(
                    v_ready, 1)

            def layer1_w2(g):
                if later(g, 1):
                    pe.wait_ge(r1_done, g)
                else:
                    pe.wait_ge(w_lo_done, len(parts))
                for n in range(2):
                    ks = range(n * KH // 2, (n + 1) * KH // 2)
                    pe.wait_ge(gzT_hi_done[n], g + 1)
                    hi_passes(y_ps, gzT_hi[:, n * BANK:(n + 1) * BANK], [w2_hi[:, k, :] for k in ks],
                              [w2_lo[:, k, :] for k in ks], n == 0)
                pe.wait_ge(gzT_lo_done[0], g + 1)
                lo_passes(y_ps, gzT_lo[:, 0:BANK], [w2_hi[:, k, :] for k in range(KH // 2)], False)

            def layer1_w2_rest(g):
                pe.wait_ge(gzT_lo_done[1], g + 1)
                lo_passes(y_ps, gzT_lo[:, BANK:DH], [w2_hi[:, k, :] for k in range(KH // 2, KH)], True).then_inc(
                    y_ready, 1)

            pe.wait_ge(ident_made, 1)
            make_G(0)
            transpose_adj(0)
            layer0(0)
            make_G(1)
            aggregate_x1(0, 0)
            transpose_adj(1)
            layer1_w1(0)

            def iteration(i, e):
                if within(i + 1, GRAPHS):
                    layer0(i + 1)
                aggregate_z(i, e)
                if within(i + 2, GRAPHS):
                    make_G(i + 2)
                if not later(i, 1):
                    spread_v()
                layer1_w2(i)
                if within(i + 1, GRAPHS):
                    aggregate_x1(i + 1, 1 - e)
                layer1_w2_rest(i)
                if within(i + 2, GRAPHS):
                    transpose_adj(i + 2)
                if within(i + 1, GRAPHS):
                    layer1_w1(i + 1)

            iteration(0, 0)
            iteration(1, 1)
            with pe.Fori(2, GRAPHS - 4, 2) as i:
                for e in range(2):
                    iteration(i + e if e else i, e)
            for i in range(GRAPHS - 4, GRAPHS):
                iteration(i, i % 2)

        @block.scalar
        def _(act):
            def relu(g, n):
                act.wait_ge(h_biased[n], g + 1)
                c = slice(n * BANK, (n + 1) * BANK)
                nc.scalar.activation(h[:, c], h[:, c], ACT.Relu).then_inc(h_relued[n], 1)

            def root_h(g):
                act.wait_ge(mvh_done, g + 1)
                if later(g, 1):
                    act.wait_ge(nbh_done, g)
                    act.wait_ge(z_done, g * 2)
                nc.scalar.activation(sdh[:, 0:1], mvh[:, 1:2], ACT.Sqrt, bias=eps_scaled[:, :],
                                     scale=PART_SCALE ** -2).then_inc(sdh_done, 1)

            def z_high(g):
                act.wait_ge(nbh_done, g + 1)
                for n in range(2):
                    if later(g, 1):
                        act.wait_ge(gz_ready[n], g)
                    c = slice(n * BANK, (n + 1) * BANK)
                    nc.scalar.activation(z_hi[:, c], h[:, c], ACT.Identity, bias=nbh[:, :], scale=sdh[:, 1:2]).then_inc(
                        z_hi_done, 1)

            def gzT_high(g):
                for n in range(2):
                    act.wait_ge(gz_ready[n], g + 1)
                    if later(g, 1):
                        act.wait_ge(y_ready, g)
                    c = slice(n * BANK, (n + 1) * BANK)
                    nc.scalar.activation(gzT_hi[:, c], gz_ps[n][:, :], ACT.Identity).then_inc(gzT_hi_done[n], 1)

            def root0(g):
                act.wait_ge(mv0_done, g + 1)
                nc.scalar.activation(sd0[:, 0:1], mv0[:, 1:2], ACT.Sqrt, bias=eps_col[:, :]).then_inc(sd0_done, 1)

            def x1_high(g, p):
                act.wait_ge(x1_done, g + 1)
                if later(g, 1):
                    act.wait_ge(gx_ready, g)
                nc.scalar.activation(x1_hi[:, :], x1[:, p, :], ACT.Identity, scale=PART_SCALE).then_inc(x1_hi_done, 1)

            def G_high(g, p):
                act.wait_ge(G_ready, g + 1)
                if later(g, 2):
                    act.wait_ge(gz_ready[1], g - 1)
                nc.scalar.activation(G_hi[:, p, :], adj_ps[:, 0:P], ACT.Identity, scale=PART_SCALE).then_inc(
                    G_hi_done, 1)

            def adjT_high(g):
                act.wait_ge(adj_transposed, g + 1)
                if later(g, 1):
                    act.wait_ge(l0_ready, g)
                nc.scalar.activation(adjT_hi[:, :], adj_ps[:, 0:P], ACT.Identity).then_inc(adjT_hi_done, 1)

            def xT_high(g, p):
                act.wait_ge(x_loaded[p], loads(g, p))
                if later(g, 1):
                    act.wait_ge(l0_ready, g)
                nc.scalar.activation(xT_hi[:, :], x_in[:, p, D:2 * D], ACT.Identity).then_inc(xT_hi_done, 1)

            def gxT_high(g):
                act.wait_ge(gx_ready, g + 1)
                if later(g, 1):
                    act.wait_ge(h_ready[1], g)
                nc.scalar.activation(gxT_hi[:, :], gx_ps[:, :], ACT.Identity).then_inc(gxT_hi_done, 1)

            def xw_high(g):
                act.wait_ge(xw_ready, g + 1)
                if later(g, 1):
                    act.wait_ge(l0_ready, g)
                nc.scalar.activation(xw_hi[:, :], xw_ps[:, :], ACT.Identity).then_inc(xw_hi_done, 1)

            def root1(g):
                act.wait_ge(mv1_done, g + 1)
                nc.scalar.activation(sd1[:, 0:1], mv1[:, 1:2], ACT.Sqrt, bias=eps_col[:, :]).then_inc(sd1_done, 1)

            def normalise_out(g, p):
                act.wait_ge(nb1_done, g + 1)
                if later(g, 2):
                    act.wait_ge(stored[p], loads(g, p) - 16)
                nc.scalar.activation(y_out[:, p, :], r1[:, :], ACT.Identity, bias=nb1[:, :], scale=sd1[:, 1:2]).then_inc(
                    y_done, 1)

            def weights_high(first, end):
                for n in range(first, end):
                    source, hi, _, k, loaded = parts[n]
                    act.wait_ge(loaded, 16)
                    if n == W2_AT:
                        act.wait_ge(scales_loaded, 16)
                    if k is None:
                        nc.scalar.activation(hi, source, ACT.Identity).then_inc(w_hi_done, 1)
                    else:
                        nc.scalar.activation(hi, source, ACT.Identity, scale=scales[:, 0, k:k + 1]).then_inc(w_hi_done, 1)

            act.wait_ge(consts, 5)
            nc.scalar.activation(root_warm[:, :], eps_col[:, :], ACT.Sqrt)
            xT_high(0, 0)
            G_high(0, 0)
            weights_high(0, 1)
            adjT_high(0)
            weights_high(1, W1_AT + 1)
            xw_high(0)
            weights_high(W1_AT + 1, W1_AT + 3)
            G_high(1, 1)
            root0(0)
            weights_high(W1_AT + 3, W2_AT)
            x1_high(0, 0)
            xT_high(1, 1)
            gxT_high(0)
            adjT_high(1)
            weights_high(W2_AT, len(parts))
            act.wait_ge(w_lo_done, W2_AT)
            for k in range(KH):
                if k == KH // 2:
                    relu(0, 0)
                nc.scalar.activation(v_terms[:, k, :], stage_a[:, k, :], ACT.Identity,
                                     scale=scales[:, 1, k:k + 1]).then_inc(v_multiplied, 1)

            def iteration(i, e):
                root_h(i)
                if within(i + 1, GRAPHS):
                    xw_high(i + 1)
                z_high(i)
                gzT_high(i)
                if within(i + 2, GRAPHS):
                    xT_high(i + 2, e)
                if within(i + 1, GRAPHS):
                    root0(i + 1)
                if within(i + 2, GRAPHS):
                    G_high(i + 2, e)
                if within(i + 1, GRAPHS):
                    x1_high(i + 1, 1 - e)
                    gxT_high(i + 1)
                if within(i + 2, GRAPHS):
                    adjT_high(i + 2)
                if within(i + 1, GRAPHS):
                    relu(i + 1, 0)
                root1(i)
                normalise_out(i, e)

            iteration(0, 0)
            iteration(1, 1)
            with act.Fori(2, GRAPHS - 4, 2) as i:
                for e in range(2):
                    iteration(i + e if e else i, e)
            for i in range(GRAPHS - 4, GRAPHS):
                iteration(i, i % 2)

        @block.vector
        def _(dve):
            def sum_adj(g, p):
                dve.wait_ge(adj_loaded[p], loads(g, p))
                nc.vector.reduce_sum(deg[:, 0:1], adj_in[:, p, 0:P], axis=AX_X).then_inc(deg_summed, 1)

            def invert_deg(g, h_stats=None):
                dve.wait_ge(deg_summed, g + 1)
                if h_stats is not None:
                    dve.wait_ge(sth_done, h_stats * 2 + 2)
                nc.vector.tensor_scalar_max(deg[:, 1:2], deg[:, 0:1], DEG_EPS).then_inc(deg_guarded, 1)
                if h_stats is not None:
                    aggregate_h()
                dve.wait_ge(deg_guarded, g + 1)
                nc.vector.reciprocal(deg[:, 2:3], deg[:, 1:2]).then_inc(deg_inverted, 1)

            def scale_adj(g, p):
                if later(g, 1):
                    dve.wait_ge(adj_transposed, g)
                dve.wait_ge(deg_inverted, g + 1)
                nc.vector.tensor_scalar_mul(adj_norm[:, :], adj_in[:, p, 0:P], deg[:, 2:3]).then_inc(adj_normed, 1)

            def incidence(g, p, stats1=None):
                dve.wait_ge(adj_loaded[p], loads(g, p))
                if later(g, 1):
                    dve.wait_ge(G_ready, g)
                if stats1 is not None:
                    dve.wait_ge(st1_done, stats1 + 1)
                nc.vector.tensor_scalar(incT[:, :], adj_in[:, p, P:2 * P], 0.0, 0.0, ALU.not_equal, ALU.add,
                                        accum_out=count[:, 0:1]).then_inc(inc_made, 1)
                if stats1 is not None:
                    aggregate1()
                nc.vector.tensor_copy(incT_be[:, P:P + 1], adj_in[:, p, P:P + 1]).then_inc(w_col_done, 1)
                dve.wait_ge(inc_made, g + 1)
                nc.vector.tensor_scalar_max(count[:, 1:2], count[:, 0:1], 1.0).then_inc(count_guarded, 1)

            def invert_count(g):
                dve.wait_ge(count_guarded, g + 1)
                nc.vector.reciprocal(count[:, 2:3], count[:, 1:2]).then_inc(count_inverted, 1)

            def scale_incidence(g):
                dve.wait_ge(count_inverted, g + 1)
                nc.vector.tensor_scalar_mul(incT_be[:, 0:P], incT[:, :], count[:, 2:3]).then_inc(inc_be_done, 1)

            def copy_G(g, p):
                dve.wait_ge(G_hi_done, g + 1)
                if later(g, 2):
                    dve.wait_ge(gz_ready[1], g - 1)
                nc.vector.scalar_tensor_tensor(out=G_lo[:, p, :], in0=adj_ps[:, 0:P], scalar=PART_SCALE,
                                               in1=G_hi[:, p, :], op0=ALU.mult, op1=ALU.subtract).then_inc(
                    G_lo_done, 1)
                if later(g, 1):
                    dve.wait_ge(dq_done, g)
                nc.vector.tensor_copy(dsum[:, :], adj_ps[:, P:P + 2]).then_inc(dsum_done, 1)

            def degrees(g):
                dve.wait_ge(dsum_done, g + 1)
                nc.vector.tensor_scalar_max(dcol[:, 0:1], dsum[:, 0:1], TINY).then_inc(d_guarded, 1)
                nc.vector.tensor_scalar(dcol[:, 1:2], dsum[:, 0:1], 0.0, PART_SCALE ** -2, ALU.is_gt,
                                        ALU.mult).then_inc(d_positive, 1)
                dve.wait_ge(d_guarded, g + 1)
                nc.vector.reciprocal(dcol[:, 2:3], dcol[:, 0:1]).then_inc(d_inverted, 1)

            def node_scale(g, p):
                dve.wait_ge(d_positive, g + 1)
                dve.wait_ge(d_inverted, g + 1)
                nc.vector.tensor_tensor(dn[:, p, 0:1], dcol[:, 1:2], dcol[:, 2:3], ALU.mult).then_inc(dn_done, 1)

            def node_bias_scale(g, p):
                dve.wait_ge(dn_done, g + 1)
                nc.vector.scalar_tensor_tensor(out=dn[:, p, 1:2], in0=dn[:, p, 0:1], scalar=PART_SCALE ** 2,
                                               in1=dsum[:, 1:2], op0=ALU.mult, op1=ALU.mult).then_inc(dq_done, 1)

            def xT_low(g, p):
                dve.wait_ge(xT_hi_done, g + 1)
                nc.vector.tensor_tensor(xT_lo[:, :], x_in[:, p, D:2 * D], xT_hi[:, :].bitcast(F32),
                                        ALU.subtract).then_inc(xT_lo_done, 1)

            def xw_low(g):
                dve.wait_ge(xw_hi_done, g + 1)
                nc.vector.tensor_tensor(xw_lo[:, :], xw_ps[:, :], xw_hi[:, :].bitcast(F32), ALU.subtract).then_inc(
                    xw_lo_done, 1)

            def adjT_low(g):
                dve.wait_ge(adjT_hi_done, g + 1)
                nc.vector.tensor_tensor(adjT_lo[:, :], adj_ps[:, 0:P], adjT_hi[:, :].bitcast(F32),
                                        ALU.subtract).then_inc(adjT_lo_done, 1)

            def gxT_low(g):
                dve.wait_ge(gxT_hi_done, g + 1)
                nc.vector.tensor_tensor(gxT_lo[:, :], gx_ps[:, :], gxT_hi[:, :].bitcast(F32),
                                        ALU.subtract).then_inc(gxT_lo_done, 1)

            def gzT_low(g, stats0=None):
                for n in range(2):
                    dve.wait_ge(gzT_hi_done[n], g + 1)
                    if stats0 is not None and n == 0:
                        dve.wait_ge(st0_done, stats0 + 1)
                    c = slice(n * BANK, (n + 1) * BANK)
                    nc.vector.tensor_tensor(gzT_lo[:, c], gz_ps[n][:, :], gzT_hi[:, c].bitcast(F32),
                                            ALU.subtract).then_inc(gzT_lo_done[n], 1)
                    if stats0 is not None and n == 0:
                        aggregate0()

            def residual0(g, p):
                dve.wait_ge(l0_ready, g + 1)
                if later(g, 1):
                    dve.wait_ge(x1_done, g)
                nc.vector.scalar_tensor_tensor(out=r0[:, :], in0=l0_ps[:, :], scalar=0.0, in1=x_in[:, p, 0:D],
                                               op0=ALU.max, op1=ALU.add).then_inc(r0_done, 1)

            def stats0(g):
                dve.wait_ge(r0_done, g + 1)
                nc.vector.bn_stats(st0[:, :], r0[:, :]).then_inc(st0_done, 1)

            def aggregate0():
                nc.vector.bn_aggr(mv0[:, :], st0[:, :]).then_inc(mv0_done, 1)

            def normalise_x1(g, p):
                dve.wait_ge(sd0_done, g + 1)
                nc.vector.reciprocal(sd0[:, 1:2], sd0[:, 0:1]).then_inc(rs0_done, 1)
                dve.wait_ge(rs0_done, g + 1)
                if later(g, 2):
                    dve.wait_ge(base_done, g - 1)
                nc.vector.tensor_scalar(x1[:, p, :], r0[:, :], mv0[:, 0:1], sd0[:, 1:2], ALU.subtract,
                                        ALU.mult).then_inc(x1_done, 1)

            def x1_low(g, p):
                dve.wait_ge(x1_hi_done, g + 1)
                nc.vector.scalar_tensor_tensor(out=x1_lo[:, :], in0=x1[:, p, :], scalar=PART_SCALE, in1=x1_hi[:, :],
                                               op0=ALU.mult, op1=ALU.subtract).then_inc(x1_lo_done, 1)

            def z_full(g):
                for n in range(2):
                    c = slice(n * BANK, (n + 1) * BANK)
                    if later(g, 1):
                        dve.wait_ge(z_lo_done, g * 2)
                    dve.wait_ge(rsh_done, g + 1)
                    nc.vector.tensor_scalar(z[:, c], h[:, c], mvh[:, 0:1], sdh[:, 1:2], ALU.subtract,
                                            ALU.mult).then_inc(z_done, 1)

            def z_low(g):
                for n in range(2):
                    c = slice(n * BANK, (n + 1) * BANK)
                    dve.wait_ge(z_done, g * 2 + 2)
                    dve.wait_ge(z_hi_done, g * 2 + (n + 1))
                    nc.vector.tensor_tensor(z_lo[:, c], z[:, c], z_hi[:, c], ALU.subtract).then_inc(z_lo_done, 1)

            def bias_h(g, p, n):
                dve.wait_ge(h_ready[n], g + 1)
                dve.wait_ge(dn_done, g + 1)
                if later(g, 1):
                    dve.wait_ge(z_hi_done, g * 2)
                    dve.wait_ge(z_done, g * 2)
                c = slice(n * BANK, (n + 1) * BANK)
                nc.vector.scalar_tensor_tensor(out=h[:, c], in0=h_ps[n][:, :], scalar=dn[:, p, 0:1], in1=b1_all[:, c],
                                               op0=ALU.mult, op1=ALU.add).then_inc(h_biased[n], 1)

            def relu1(g):
                dve.wait_ge(h_biased[1], g + 1)
                nc.vector.tensor_scalar_max(h[:, BANK:DH], h[:, BANK:DH], 0.0).then_inc(h_relued[1], 1)

            def stats_h(g, n):
                dve.wait_ge(h_relued[n], g + 1)
                nc.vector.bn_stats(sth[:, n, :], h[:, n * BANK:(n + 1) * BANK]).then_inc(sth_done, 1)

            def aggregate_h():
                nc.vector.bn_aggr(mvh[:, :], sth[:, :, :].rearrange("p a b -> p (a b)")).then_inc(mvh_done, 1)

            def scales_h(g):
                dve.wait_ge(sdh_done, g + 1)
                nc.vector.reciprocal(sdh[:, 1:2], sdh[:, 0:1]).then_inc(rsh_done, 1)
                dve.wait_ge(rsh_done, g + 1)
                nc.vector.scalar_tensor_tensor(out=nbh[:, :], in0=mvh[:, 0:1], scalar=-1.0, in1=sdh[:, 1:2],
                                               op0=ALU.mult, op1=ALU.mult).then_inc(nbh_done, 1)

            def base(g, p):
                dve.wait_ge(dq_done, g + 1)
                if later(g, 1):
                    dve.wait_ge(base_done, g)
                nc.vector.scalar_tensor_tensor(out=bias_y[:, :], in0=v_all[:, :], scalar=dn[:, p, 1:2], in1=b2_all[:, :],
                                               op0=ALU.mult, op1=ALU.add).then_inc(bias_done, 1)
                dve.wait_ge(bias_done, g + 1)
                dve.wait_ge(x1_done, g + 1)
                if later(g, 1):
                    dve.wait_ge(r1_done, g)
                nc.vector.scalar_tensor_tensor(out=base_y[:, :], in0=x1[:, p, :], scalar=2.0, in1=bias_y[:, :],
                                               op0=ALU.mult, op1=ALU.add).then_inc(base_done, 1)

            def residual1(g, p):
                dve.wait_ge(y_ready, g + 1)
                dve.wait_ge(base_done, g + 1)
                if later(g, 1):
                    dve.wait_ge(y_done, g)
                nc.vector.scalar_tensor_tensor(out=r1[:, :], in0=y_ps[:, :], scalar=dn[:, p, 0:1], in1=base_y[:, :],
                                               op0=ALU.mult, op1=ALU.add).then_inc(r1_done, 1)
                dve.wait_ge(r1_done, g + 1)
                nc.vector.bn_stats(st1[:, :], r1[:, :]).then_inc(st1_done, 1)

            def aggregate1():
                nc.vector.bn_aggr(mv1[:, :], st1[:, :]).then_inc(mv1_done, 1)

            def scales1(g):
                dve.wait_ge(sd1_done, g + 1)
                nc.vector.reciprocal(sd1[:, 1:2], sd1[:, 0:1]).then_inc(rs1_done, 1)
                dve.wait_ge(rs1_done, g + 1)
                nc.vector.scalar_tensor_tensor(out=nb1[:, :], in0=mv1[:, 0:1], scalar=-1.0, in1=sd1[:, 1:2],
                                               op0=ALU.mult, op1=ALU.mult).then_inc(nb1_done, 1)

            def weights_low(first, end):
                for n in range(first, end):
                    source, hi, lo, k, _ = parts[n]
                    dve.wait_ge(w_hi_done, n + 1)
                    if k is None:
                        nc.vector.tensor_tensor(lo, source, hi.bitcast(F32), ALU.subtract).then_inc(w_lo_done, 1)
                    else:
                        nc.vector.scalar_tensor_tensor(out=lo, in0=source, scalar=scales[:, 0, k:k + 1],
                                                       in1=hi.bitcast(F32), op0=ALU.mult,
                                                       op1=ALU.subtract).then_inc(w_lo_done, 1)

            dve.wait_ge(consts, 5)
            incidence(0, 0)
            invert_count(0)
            scale_incidence(0)
            sum_adj(0, 0)
            invert_deg(0)
            scale_adj(0, 0)
            xT_low(0, 0)
            copy_G(0, 0)
            weights_low(0, 1)
            adjT_low(0)
            weights_low(1, W1_AT)
            incidence(1, 1)
            sum_adj(1, 1)
            invert_count(1)
            invert_deg(1)
            scale_incidence(1)
            scale_adj(1, 1)
            xw_low(0)
            weights_low(W1_AT, W1_AT + 1)
            residual0(0, 0)
            stats0(0)
            degrees(0)
            dve.wait_ge(st0_done, 1)
            aggregate0()
            weights_low(W1_AT + 1, W1_AT + 2)
            normalise_x1(0, 0)
            weights_low(W1_AT + 2, W1_AT + 3)
            x1_low(0, 0)
            node_scale(0, 0)
            node_bias_scale(0, 0)
            copy_G(1, 1)
            weights_low(W1_AT + 3, W2_AT)
            gxT_low(0)
            xT_low(1, 1)
            adjT_low(1)
            weights_low(W2_AT, W2_AT + KH // 2)
            dve.wait_ge(bias_loaded, 32)

            def iteration(i, e):
                bias_h(i, e, 0)
                if within(i + 2, GRAPHS):
                    incidence(i + 2, e, stats1=i - 1 if later(i, 1) else None)
                    sum_adj(i + 2, e)
                    invert_count(i + 2)
                else:
                    dve.wait_ge(st1_done, i)
                    aggregate1()
                if not later(i, 1):
                    weights_low(W2_AT + KH // 2, len(parts))
                stats_h(i, 0)
                if within(i + 2, GRAPHS):
                    scale_incidence(i + 2)
                if later(i, 1):
                    scales1(i - 1)
                bias_h(i, e, 1)
                relu1(i)
                stats_h(i, 1)
                if within(i + 2, GRAPHS):
                    invert_deg(i + 2, h_stats=i)
                else:
                    dve.wait_ge(sth_done, i * 2 + 2)
                    aggregate_h()
                if within(i + 1, GRAPHS):
                    degrees(i + 1)
                scales_h(i)
                z_full(i)
                if within(i + 1, GRAPHS):
                    xw_low(i + 1)
                z_low(i)
                if within(i + 1, GRAPHS):
                    residual0(i + 1, 1 - e)
                    node_scale(i + 1, 1 - e)
                    stats0(i + 1)
                    node_bias_scale(i + 1, 1 - e)
                    gzT_low(i, stats0=i + 1)
                else:
                    gzT_low(i)
                if not later(i, 1):
                    dve.wait_ge(v_ready, 1)
                    nc.vector.tensor_copy(v_all[:, :], gx_ps[:, :]).then_inc(v_copied, 1)
                if within(i + 1, GRAPHS):
                    normalise_x1(i + 1, 1 - e)
                if within(i + 2, GRAPHS):
                    xT_low(i + 2, e)
                if within(i + 1, GRAPHS):
                    x1_low(i + 1, 1 - e)
                if within(i + 2, GRAPHS):
                    copy_G(i + 2, e)
                    scale_adj(i + 2, e)
                if not later(i, 1):
                    dve.wait_ge(v_copied, 1)
                base(i, e)
                if within(i + 1, GRAPHS):
                    gxT_low(i + 1)
                residual1(i, e)
                if within(i + 2, GRAPHS):
                    adjT_low(i + 2)

            iteration(0, 0)
            iteration(1, 1)
            with dve.Fori(2, GRAPHS - 4, 2) as i:
                for e in range(2):
                    iteration(i + e if e else i, e)
            for i in range(GRAPHS - 4, GRAPHS):
                iteration(i, i % 2)
            dve.wait_ge(st1_done, GRAPHS)
            aggregate1()
            scales1(GRAPHS - 1)


def kernel(**inputs):
    import numpy as np
    import concourse.bacc as bacc
    from concourse.bass_utils import run_bass_kernel_spmd

    x, adj = np.asarray(inputs["x"]), np.asarray(inputs["adj"])
    graphs, nodes, d = x.shape
    columns = lambda a: np.asarray(a).reshape(-1, P).T
    xT = x.reshape(graphs, nodes, d // P, P).transpose(0, 3, 2, 1).reshape(graphs, P, d // P * nodes)
    laid_out = {
        "x_pair": np.concatenate([x, xT], axis=2),
        "adj_pair": np.concatenate([adj, adj.transpose(0, 2, 1)], axis=2),
        "W0T": np.asarray(inputs["L0_gnn_W"]).T,
        "W1T": np.asarray(inputs["L1_gnn_W1"]).T,
        "b1": inputs["L1_gnn_b1"],
        "gamma_beta": np.concatenate([columns(inputs["L1_gnn_gamma"]), columns(inputs["L1_gnn_beta"])], axis=1),
        "W2T": np.asarray(inputs["L1_gnn_W2"]).T,
        "b2": inputs["L1_gnn_b2"],
    }
    nc = bacc.Bacc("TRN2", target_bir_lowering=False, num_devices=1)
    arrays, args = {}, []
    for name, a in laid_out.items():
        a = np.ascontiguousarray(a)
        arrays[f"in_{name}"] = a
        args.append(nc.dram_tensor(f"in_{name}", a.shape, mybir.dt.from_np(a.dtype), kind="ExternalInput").ap())
    out = nc.dram_tensor("out_0", x.shape, F32, kind="ExternalOutput").ap()
    two_layer_graph_kernel(nc, *args, out)
    r = run_bass_kernel_spmd(nc, [arrays], core_ids=[0])
    return r.results[0]["out_0"]
```
